# Optimizing a Trainium2 kernel written in Bass

```python
import numpy as np
import jax
import jax.numpy as jnp

def _softmax(x, axis=-1):
    return jax.nn.softmax(x, axis=axis)

def _gelu(x):
    return jax.nn.gelu(x, approximate=True)

def _silu(x):
    return jax.nn.silu(x)

def _sigmoid(x):
    return jax.nn.sigmoid(x)

def _layernorm(x, axis=-1, eps=1e-05):
    m = jnp.mean(x, axis=axis, keepdims=True)
    v = jnp.var(x, axis=axis, keepdims=True)
    return (x - m) / jnp.sqrt(v + eps)

def _scatter_add(tgt, idx, src, axis=0):
    return tgt.at[idx].add(src)

def _segment_sum(src, seg, n):
    return jax.ops.segment_sum(src, seg, n)
kernel_name = 'mk_vit_tower_d2_tok_img1024_r4_b70168'

def setup_inputs(seed: int=0):
    np.random.seed(seed)
    _w = jnp.asarray

    def _rec_inputs():
        import jax
        import jax.numpy as jnp
        _rk = jax.random.key(seed)
        x = -0.000348323 + 0.999952 * jax.random.normal(jax.random.fold_in(_rk, 1), (16, 3, 96, 96), jnp.float32)
        return x
    x = _rec_inputs()

    def _L0_tok_setup():
        import jax, jax.numpy as jnp
        import numpy as np
        from jax import lax
        PATCH = 16
        key = jax.random.key(seed)
        k1, k2 = jax.random.split(key)
        B, C, IMG, HID = (32, 3, 96, 256)
        inputs = jax.random.normal(k1, (B, C, IMG, IMG), dtype=jnp.float32)
        flat = C * PATCH * PATCH
        W = jax.random.normal(k2, (flat, HID), dtype=jnp.float32) / np.sqrt(flat)
        return {'inputs': inputs, 'W': W}
    _L0_tok_all = _L0_tok_setup()
    _L0_tok_in = {k: v for k, v in _L0_tok_all.items() if k in ('W',)}
    del _L0_tok_all

    def _L0_attn_setup():
        import jax, jax.numpy as jnp
        import numpy as np
        D_IN = 256
        D_OUT = 256
        H = 16
        G = 4
        LF = 2
        HEAD_OUT = D_OUT // H
        DQ = HEAD_OUT // LF
        B, T = (2, 512)

        def _alibi_bias(T, dtype):
            slopes = jnp.asarray(2.0 ** (-8.0 * np.arange(1, H + 1) / H), dtype=dtype)
            pos = jnp.arange(T)
            rel = (pos[None, :] - pos[:, None]).astype(dtype)
            return slopes[:, None, None] * rel[None, :, :]
        key = jax.random.key(seed)
        ks = jax.random.split(key, 7)
        s = 0.02
        return {'x': jax.random.normal(ks[0], (B, T, D_IN), dtype=jnp.float32), 'Wq': jax.random.normal(ks[1], (D_IN, D_OUT // LF), dtype=jnp.float32) * s, 'Wk': jax.random.normal(ks[2], (D_IN, D_OUT // LF // G), dtype=jnp.float32) * s, 'Wv': jax.random.normal(ks[3], (D_IN, D_OUT // G), dtype=jnp.float32) * s, 'Wp': jax.random.normal(ks[4], (D_OUT, D_OUT), dtype=jnp.float32) * s, 'bp': jnp.zeros((D_OUT,), dtype=jnp.float32)}
    _L0_attn_all = _L0_attn_setup()
    _L0_attn_in = {k: v for k, v in _L0_attn_all.items() if k in ('Wq', 'Wk', 'Wv', 'Wp', 'bp')}
    del _L0_attn_all

    def _L0_ffn_setup():
        import jax, jax.numpy as jnp
        import numpy as np
        B, S, H, E, K = (2, 256, 256, 8, 2)
        F = 4 * H
        key = jax.random.key(seed)
        ks = jax.random.split(key, 8)
        std = 0.02
        return {'x': jax.random.normal(ks[0], (B, S, H), jnp.float32), 'gate_w': jax.random.normal(ks[1], (E, H), jnp.float32) * (std / np.sqrt(H)), 'gate_bias': jnp.zeros((E,), jnp.float32), 'Wu': jax.random.normal(ks[2], (E, F, H), jnp.float32) * std, 'bu': jnp.zeros((E, F), jnp.float32), 'Wd': jax.random.normal(ks[3], (E, H, F), jnp.float32) * std, 'bd': jnp.zeros((E, H), jnp.float32), 'sWu': jax.random.normal(ks[4], (F, H), jnp.float32) * std, 'sbu': jnp.zeros((F,), jnp.float32), 'sWd': jax.random.normal(ks[5], (H, F), jnp.float32) * std, 'sbd': jnp.zeros((H,), jnp.float32)}
    _L0_ffn_all = _L0_ffn_setup()
    _L0_ffn_in = {k: v for k, v in _L0_ffn_all.items() if k in ('gate_w', 'gate_bias', 'Wu', 'bu', 'Wd', 'bd', 'sWu', 'sbu', 'sWd', 'sbd')}
    del _L0_ffn_all

    def _L1_attn_setup():
        import math
        import jax, jax.numpy as jnp
        import numpy as np
        D_MODEL = 256
        HEADS = 16
        DH = D_MODEL // HEADS
        MAX_REL = 128
        LN_EPS = 1e-05

        def _layernorm(x, gamma, beta):
            mu = jnp.mean(x, axis=-1, keepdims=True)
            var = jnp.mean(jnp.square(x - mu), axis=-1, keepdims=True)
            return (x - mu) * jax.lax.rsqrt(var + LN_EPS) * gamma + beta
        key = jax.random.key(seed)
        ks = jax.random.split(key, 6)
        B, T = (4, 512)
        scale = 1.0 / math.sqrt(D_MODEL)
        x = jax.random.normal(ks[0], (B, T, D_MODEL), dtype=jnp.float32)
        Wq = jax.random.normal(ks[1], (D_MODEL, D_MODEL), dtype=jnp.float32) * scale
        Wk = jax.random.normal(ks[2], (D_MODEL, D_MODEL), dtype=jnp.float32) * scale
        Wv = jax.random.normal(ks[3], (D_MODEL, D_MODEL), dtype=jnp.float32) * scale
        Wo = jax.random.normal(ks[4], (D_MODEL, D_MODEL), dtype=jnp.float32) * scale
        rel = jnp.tile(jnp.linspace(0.0, -2.0, MAX_REL + 1, dtype=jnp.float32)[None, :], (HEADS, 1))
        ln_gamma = jnp.ones((D_MODEL,), dtype=jnp.float32)
        ln_beta = jnp.zeros((D_MODEL,), dtype=jnp.float32)
        return {'x': x, 'Wq': Wq, 'Wk': Wk, 'Wv': Wv, 'Wo': Wo, 'rel': rel, 'ln_gamma': ln_gamma, 'ln_beta': ln_beta}
    _L1_attn_all = _L1_attn_setup()
    _L1_attn_in = {k: v for k, v in _L1_attn_all.items() if k in ('Wq', 'Wk', 'Wv', 'Wo', 'rel', 'ln_gamma', 'ln_beta')}
    del _L1_attn_all

    def _L1_ffn_setup():
        import jax, jax.numpy as jnp
        import numpy as np
        TOP_K = 2
        ROUTE_SCALE = 1.0
        EPS = 1e-20
        key = jax.random.key(seed)
        ks = jax.random.split(key, 8)
        dim, hid, E, X = (256, 704, 8, 1)
        std = 0.02
        x = jax.random.normal(ks[0], (2, 512, dim), dtype=jnp.float32)
        w1 = jax.random.normal(ks[1], (E, hid, dim), dtype=jnp.float32) * std
        w2 = jax.random.normal(ks[2], (E, dim, hid), dtype=jnp.float32) * std
        w3 = jax.random.normal(ks[3], (E, hid, dim), dtype=jnp.float32) * std
        new_w1 = jax.random.normal(ks[4], (X, hid, dim), dtype=jnp.float32) * std
        new_w2 = jnp.zeros((X, dim, hid), dtype=jnp.float32)
        new_w3 = jax.random.normal(ks[5], (X, hid, dim), dtype=jnp.float32) * std
        gate_weight = jax.random.normal(ks[6], (E, dim), dtype=jnp.float32) * std
        new_gate_weight = jax.random.normal(ks[7], (X, dim), dtype=jnp.float32) * std
        gate_bias = jnp.zeros((X,), dtype=jnp.float32)
        return dict(x=x, w1=w1, w2=w2, w3=w3, new_w1=new_w1, new_w2=new_w2, new_w3=new_w3, gate_weight=gate_weight, new_gate_weight=new_gate_weight, gate_bias=gate_bias)
    _L1_ffn_all = _L1_ffn_setup()
    _L1_ffn_in = {k: v for k, v in _L1_ffn_all.items() if k in ('w1', 'w2', 'w3', 'new_w1', 'new_w2', 'new_w3', 'gate_weight', 'new_gate_weight', 'gate_bias')}
    del _L1_ffn_all
    return {'x': x, 'L0_tok_W': _L0_tok_in['W'], 'L0_attn_Wq': _L0_attn_in['Wq'], 'L0_attn_Wk': _L0_attn_in['Wk'], 'L0_attn_Wv': _L0_attn_in['Wv'], 'L0_attn_Wp': _L0_attn_in['Wp'], 'L0_attn_bp': _L0_attn_in['bp'], 'L0_ffn_gate_w': _L0_ffn_in['gate_w'], 'L0_ffn_gate_bias': _L0_ffn_in['gate_bias'], 'L0_ffn_Wu': _L0_ffn_in['Wu'], 'L0_ffn_bu': _L0_ffn_in['bu'], 'L0_ffn_Wd': _L0_ffn_in['Wd'], 'L0_ffn_bd': _L0_ffn_in['bd'], 'L0_ffn_sWu': _L0_ffn_in['sWu'], 'L0_ffn_sbu': _L0_ffn_in['sbu'], 'L0_ffn_sWd': _L0_ffn_in['sWd'], 'L0_ffn_sbd': _L0_ffn_in['sbd'], 'L1_attn_Wq': _L1_attn_in['Wq'], 'L1_attn_Wk': _L1_attn_in['Wk'], 'L1_attn_Wv': _L1_attn_in['Wv'], 'L1_attn_Wo': _L1_attn_in['Wo'], 'L1_attn_rel': _L1_attn_in['rel'], 'L1_attn_ln_gamma': _L1_attn_in['ln_gamma'], 'L1_attn_ln_beta': _L1_attn_in['ln_beta'], 'L1_ffn_w1': _L1_ffn_in['w1'], 'L1_ffn_w2': _L1_ffn_in['w2'], 'L1_ffn_w3': _L1_ffn_in['w3'], 'L1_ffn_new_w1': _L1_ffn_in['new_w1'], 'L1_ffn_new_w2': _L1_ffn_in['new_w2'], 'L1_ffn_new_w3': _L1_ffn_in['new_w3'], 'L1_ffn_gate_weight': _L1_ffn_in['gate_weight'], 'L1_ffn_new_gate_weight': _L1_ffn_in['new_gate_weight'], 'L1_ffn_gate_bias': _L1_ffn_in['gate_bias']}

def reference(x, L0_tok_W, L0_attn_Wq, L0_attn_Wk, L0_attn_Wv, L0_attn_Wp, L0_attn_bp, L0_ffn_gate_w, L0_ffn_gate_bias, L0_ffn_Wu, L0_ffn_bu, L0_ffn_Wd, L0_ffn_bd, L0_ffn_sWu, L0_ffn_sbu, L0_ffn_sWd, L0_ffn_sbd, L1_attn_Wq, L1_attn_Wk, L1_attn_Wv, L1_attn_Wo, L1_attn_rel, L1_attn_ln_gamma, L1_attn_ln_beta, L1_ffn_w1, L1_ffn_w2, L1_ffn_w3, L1_ffn_new_w1, L1_ffn_new_w2, L1_ffn_new_w3, L1_ffn_gate_weight, L1_ffn_new_gate_weight, L1_ffn_gate_bias):
    import jax
    import jax.numpy as jnp

    def _L0_tok_ref(inputs, W):
        import jax, jax.numpy as jnp
        import numpy as np
        from jax import lax
        PATCH = 16
        B, C, H, Wimg = inputs.shape
        patches = lax.conv_general_dilated_patches(inputs, filter_shape=[PATCH, PATCH], window_strides=[PATCH, PATCH], padding='VALID', dimension_numbers=('NCHW', 'HWIO', 'NCHW'))
        patches = patches.reshape(B, -1, C * PATCH * PATCH)
        return jnp.einsum('bnf,fh->bnh', patches, W)

    def _L0_attn_ref(x, Wq, Wk, Wv, Wp, bp):
        import jax, jax.numpy as jnp
        import numpy as np
        D_IN = 256
        D_OUT = 256
        H = 16
        G = 4
        LF = 2
        HEAD_OUT = D_OUT // H
        DQ = HEAD_OUT // LF
        B, T = (2, 512)

        def _alibi_bias(T, dtype):
            slopes = jnp.asarray(2.0 ** (-8.0 * np.arange(1, H + 1) / H), dtype=dtype)
            pos = jnp.arange(T)
            rel = (pos[None, :] - pos[:, None]).astype(dtype)
            return slopes[:, None, None] * rel[None, :, :]
        b, t, _ = x.shape
        q = x @ Wq
        k = jnp.tile(x @ Wk, (1, 1, G))
        v = jnp.tile(x @ Wv, (1, 1, G))
        q = q.reshape(b, t, H, DQ).transpose(0, 2, 1, 3)
        k = k.reshape(b, t, H, DQ).transpose(0, 2, 1, 3)
        v = v.reshape(b, t, H, HEAD_OUT).transpose(0, 2, 1, 3)
        scores = jnp.einsum('bhqd,bhkd->bhqk', q, k)
        causal = jnp.triu(jnp.ones((t, t), dtype=bool), k=1)
        scores = jnp.where(causal, -jnp.inf, scores)
        scores = (scores + _alibi_bias(t, scores.dtype)) / jnp.sqrt(jnp.asarray(DQ, scores.dtype))
        w = jax.nn.softmax(scores, axis=-1)
        ctx = jnp.einsum('bhqk,bhkd->bqhd', w, v).reshape(b, t, D_OUT)
        return ctx @ Wp + bp

    def _L0_ffn_ref(x, gate_w, gate_bias, Wu, bu, Wd, bd, sWu, sbu, sWd, sbd):
        import jax, jax.numpy as jnp
        import numpy as np
        B, S, H, E, K = (2, 256, 256, 8, 2)
        F = 4 * H
        b, s, h = x.shape
        x_flat = x.reshape(-1, h)
        T = x_flat.shape[0]
        scores = jax.nn.sigmoid(x_flat @ gate_w.T + gate_bias)
        top_scores, top_idx = jax.lax.top_k(scores, K)
        top_scores = top_scores / (top_scores.sum(-1, keepdims=True) + 1e-06)
        w = jnp.zeros((T, E), x.dtype).at[jnp.arange(T)[:, None], top_idx].add(top_scores)
        h1 = jnp.einsum('th,efh->etf', x_flat, Wu) + bu[:, None, :]
        a1 = jax.nn.gelu(h1, approximate=False)
        y = jnp.einsum('etf,ehf->eth', a1, Wd) + bd[:, None, :]
        combined = jnp.einsum('te,eth->th', w, y)
        sh = jax.nn.gelu(x_flat @ sWu.T + sbu, approximate=False)
        shared = (sh @ sWd.T + sbd) * 0.1
        return (combined + shared).reshape(b, s, h)

    def _L1_attn_ref(x, Wq, Wk, Wv, Wo, rel, ln_gamma, ln_beta):
        import math
        import jax, jax.numpy as jnp
        import numpy as np
        D_MODEL = 256
        HEADS = 16
        DH = D_MODEL // HEADS
        MAX_REL = 128
        LN_EPS = 1e-05

        def _layernorm(x, gamma, beta):
            mu = jnp.mean(x, axis=-1, keepdims=True)
            var = jnp.mean(jnp.square(x - mu), axis=-1, keepdims=True)
            return (x - mu) * jax.lax.rsqrt(var + LN_EPS) * gamma + beta
        B, T, D = x.shape
        x0 = x
        xn = _layernorm(x, ln_gamma, ln_beta)

        def proj(W):
            return (xn @ W.T).reshape(B, T, HEADS, DH).transpose(0, 2, 1, 3)
        q = proj(Wq) / math.sqrt(DH)
        k = proj(Wk)
        v = proj(Wv)
        scores = jnp.einsum('bhid,bhjd->bhij', q, k)
        i = jnp.arange(T)
        dist = jnp.clip(i[:, None] - i[None, :], 0, MAX_REL)
        bias = rel[:, dist]
        scores = scores + bias[None]
        causal = i[:, None] >= i[None, :]
        scores = jnp.where(causal[None, None], scores, -jnp.inf)
        attn = jax.nn.softmax(scores, axis=-1)
        y = jnp.einsum('bhij,bhjd->bhid', attn, v)
        y = y.transpose(0, 2, 1, 3).reshape(B, T, D)
        y = y @ Wo.T
        return x0 + y

    def _L1_ffn_ref(x, w1, w2, w3, new_w1, new_w2, new_w3, gate_weight, new_gate_weight, gate_bias):
        import jax, jax.numpy as jnp
        import numpy as np
        TOP_K = 2
        ROUTE_SCALE = 1.0
        EPS = 1e-20
        bs, slen, dim = x.shape
        x_flat = x.reshape(-1, dim)
        ew1 = jnp.concatenate([w1, new_w1], axis=0)
        ew2 = jnp.concatenate([w2, new_w2], axis=0)
        ew3 = jnp.concatenate([w3, new_w3], axis=0)
        gate = jnp.concatenate([gate_weight, new_gate_weight], axis=0)
        e_orig = w1.shape[0]
        e_tot = gate.shape[0]
        bias = jnp.concatenate([jnp.zeros((e_orig,), x.dtype), gate_bias])
        scores = jax.nn.sigmoid((x_flat @ gate.T + bias).astype(jnp.float32))
        top_scores, selected = jax.lax.top_k(scores, TOP_K)
        top_scores = top_scores / (jnp.sum(top_scores, axis=-1, keepdims=True) + EPS)
        top_scores = top_scores * ROUTE_SCALE
        onehot = jax.nn.one_hot(selected, e_tot, dtype=jnp.float32)
        cw = jnp.einsum('tk,tke->te', top_scores, onehot)
        out = jnp.zeros_like(x_flat)
        for e in range(e_tot):
            h = jax.nn.silu(x_flat @ ew1[e].T) * (x_flat @ ew3[e].T)
            out = out + cw[:, e:e + 1] * (h @ ew2[e].T)
        return out.reshape(bs, slen, dim)
    h = _L0_tok_ref(x, L0_tok_W)
    h = h + _L0_attn_ref(_layernorm(h, axis=-1), L0_attn_Wq, L0_attn_Wk, L0_attn_Wv, L0_attn_Wp, L0_attn_bp)
    h = h + _L0_ffn_ref(_layernorm(h, axis=-1), L0_ffn_gate_w, L0_ffn_gate_bias, L0_ffn_Wu, L0_ffn_bu, L0_ffn_Wd, L0_ffn_bd, L0_ffn_sWu, L0_ffn_sbu, L0_ffn_sWd, L0_ffn_sbd)
    h = h + _L1_attn_ref(_layernorm(h, axis=-1), L1_attn_Wq, L1_attn_Wk, L1_attn_Wv, L1_attn_Wo, L1_attn_rel, L1_attn_ln_gamma, L1_attn_ln_beta)
    h = h + _L1_ffn_ref(_layernorm(h, axis=-1), L1_ffn_w1, L1_ffn_w2, L1_ffn_w3, L1_ffn_new_w1, L1_ffn_new_w2, L1_ffn_new_w3, L1_ffn_gate_weight, L1_ffn_new_gate_weight, L1_ffn_gate_bias)
    return h

_drawn_inputs = setup_inputs


def setup_inputs(seed=0):
    import zlib

    import numpy as np

    out = dict(_drawn_inputs(seed))
    spreads = {'L0_attn_bp': (0.0, 0.1),
     'L0_ffn_gate_bias': (0.0, 0.1),
     'L0_ffn_bu': (0.0, 0.284),
     'L0_ffn_bd': (0.0, 0.1),
     'L0_ffn_sbu': (0.0, 0.8),
     'L0_ffn_sbd': (0.0, 0.692),
     'L1_attn_ln_gamma': (1.0, 0.2),
     'L1_attn_ln_beta': (0.0, 0.1),
     'L1_ffn_new_w2': (0.0, 0.476)}
    factors = {'L0_attn_Wq': 8.0,
     'L0_attn_Wk': 8.0,
     'L0_ffn_sWu': 5.062,
     'L0_ffn_sWd': 4.633,
     'L1_attn_rel': 8.0,
     'L1_ffn_w1': 6.29,
     'L1_ffn_w2': 6.128,
     'L1_ffn_w3': 6.136,
     'L1_ffn_new_w1': 3.384,
     'L1_ffn_new_w3': 3.355,
     'L1_ffn_gate_weight': 4.412,
     'L1_ffn_new_gate_weight': 4.004}
    for name, (base, spread) in spreads.items():
        noise = np.random.default_rng([zlib.crc32(name.encode()), seed]).standard_normal(out[name].shape)
        drawn = base * np.exp(spread * noise) if base else spread * noise
        out[name] = jnp.asarray(drawn.astype(out[name].dtype))
    for name, factor in factors.items():
        out[name] = (out[name] * factor).astype(out[name].dtype)
    return out
```

```python
from contextlib import ExitStack

import concourse.bass as bass
from concourse import mybir

F32 = mybir.dt.float32
BF16 = mybir.dt.bfloat16
I32 = mybir.dt.int32
U32 = mybir.dt.uint32
ACT = mybir.ActivationFunctionType
ALU = mybir.AluOpType
AX = mybir.AxisListType.X

P = 128
IMGS, PATCHES, D, FEAT = 16, 36, 256, 768
TOK = IMGS * PATCHES
NT = -(-TOK // P)
ROWS = [min(P, TOK - t * P) for t in range(NT)]
HALF = TOK // 2
PAIRS = IMGS // 2
HEADS, DH = 16, 16
DQ = (8, 16)
KCHUNKS = (1, 4)
VCOLS = (64, 256)
QSCALE = (8.0 ** -0.5, 16.0 ** -0.5)
GROUPS = [(3 * g, min(3, HEADS - 3 * g)) for g in range(-(-HEADS // 3))]
VW = DH + 1
EPS_LN = 1e-5
EXPERTS = (8, 9)
HID = (1024, 704)
FCH = (8, 6)
SEG = (512, 352)
BLOCKS = tuple((2 * TOK + e * (P - 1)) // P for e in EXPERTS)
ALWAYS = -(-2 * TOK // P)
BLOCKS_USED = 18
SLOT = 4352
EPS_TOPK = (1e-6, 1e-20)
FIRST_SLOT = (1, 0)
NEG = -1e30

CONST = {}
_at = 0
for _name, _n in (("ident", P), ("tri", P), ("vmask", HEADS), ("le0", 64), ("le1", 81), ("thr", NT),
                  ("valid", NT), ("ids", 9), ("blk", 18)):
    CONST[_name] = (_at, _n)
    _at += _n
NCONST = _at


def dims(ap, *shape):
    names = "abcd"[:len(shape)]
    return ap.rearrange(f"p ({' '.join(names)}) -> p {' '.join(names)}", **dict(zip(names, shape)))


def tower(nc, a, out):
    ctx = ExitStack()
    with ctx:
        def sb(name, shape, dt=F32):
            return ctx.enter_context(nc.sbuf_tensor(name, shape, dt))

        def sem(name):
            return ctx.enter_context(nc.semaphore(name))

        def sem2(name):
            return [sem(f"{name}_{n}") for n in range(2)]

        W = sb("expert_slots", [P, 9 * SLOT])
        R1 = sb("phase_buffers", [P, 4864])
        R2 = sb("row_buffers", [P, 1024])
        wA = sb("attn_weights", [P, 3072])
        h_t = sb("h", [P, NT * D])
        x_t = sb("xln", [P, NT * D])
        xnT_t = sb("xnT", [P, 2 * TOK])
        cst = sb("consts", [P, NCONST])
        sel = sb("bias_select", [9, 3, P], BF16)
        small = sb("small", [P, 100])
        rt = sb("route", [P, 10 * 45])
        pos_i = sb("positions", [P, 2, NT], I32)
        be_i = sb("block_slots", [1, BLOCKS_USED + 1], I32)
        pw = sb("pair_weights", [P, 2, NT])
        gateT = sb("gateT", [P, 2, 9])
        gbias = sb("gate_bias", [P, 9])

        h = dims(h_t[:, :], NT, D)
        xln = dims(x_t[:, :], NT, D)
        xnT = dims(xnT_t[:, :], 2, TOK)

        def slot(s, off, n):
            return W[:, s * SLOT + off:s * SLOT + off + n]

        def const(name):
            o, n = CONST[name]
            return cst[:, o:o + n]

        ident = const("ident")
        vblk = dims(slot(7, 0, IMGS * HEADS * VW), IMGS, HEADS, VW)
        qT = dims(slot(8, 0, 4 * TOK), 4, TOK)
        pT = [dims(slot(8, 2304 + 432 * i, 432), 6, 72) for i in range(2)]
        abias = slot(8, 2304 + 864, 576)
        kT = dims(R1[:, 0:4 * TOK], 4, TOK)
        xln2 = dims(R1[:, 0:NT * D], NT, D)
        x3 = [dims(t, IMGS, 3, PATCHES) for t in (R1[:, 2304:2304 + 3 * TOK], slot(8, 2304, 3 * TOK))]
        ctxT = dims(R1[:, 2304:2304 + 2 * TOK], 2, TOK)
        prob = [R1[:, 3456 + 576 * i:3456 + 576 * (i + 1)] for i in range(2)]
        ctxn = [R2[:, 256 * i:256 * (i + 1)] for i in range(2)]
        zeros = R2[:, 0:256]
        bp = R2[:, 768:1024]
        wq = dims(wA[:, 0:1024], 2, 512)
        wk = [dims(wA[:, 1024:1024 + 256], 2, 128), dims(wA[:, 1024:2048], 2, 512)]
        wv = [dims(wA[:, 2048:2048 + 128], 2, 64), dims(wA[:, 2048:2560], 2, 256)]
        wo = dims(wA[:, 2560:3072], 2, 256)
        patch = dims(slot(7, 0, 6 * TOK), 6, TOK)
        tokw = dims(slot(8, 0, 6 * D), 6, D)
        shT = dims(R1[:, 0:8 * TOK], 8, TOK)
        sbd = R1[:, 4608:4864]
        act = [R1[:, 1024 * i:1024 * (i + 1)] for i in range(2)]
        actT = R1[:, 2048:3072]
        ys = [R1[:, 3072 + 256 * i:3072 + 256 * (i + 1)] for i in range(2)]
        back = dims(R1[:, 0:2 * NT * D], 2, NT, D)
        xb = [R2[:, 256 * i:256 * (i + 1)] for i in range(2)]
        xbT = [dims(R2[:, 512 + 256 * i:512 + 256 * (i + 1)], 2, P) for i in range(2)]
        braw = R1[:, 0:96]
        brest = R1[:, 96:192]
        bparts = [R1[:, 192 + 48 * i:192 + 48 * (i + 1)].bitcast(BF16) for i in range(3)]
        selraw = dims(R1[0:9, 512:512 + 3 * P], 3, P)
        stats = dims(small[:, 0:30], NT, 6)
        mv = dims(small[:, 30:40], NT, 2)
        ve = small[:, 40:45]
        rstd = small[:, 45:50]
        mhalf = small[:, 50:55]
        nmax = small[:, 55:71]
        rinv = small[:, 71:87]
        one = small[:, 87:88]
        sbu = small[:, 88:96]
        gb = small[:, 96:100]

        PS = ctx.enter_context(nc.psum_tensor("psum", [P, 8, 512], F32))
        ps_flat = PS[:, :, :].rearrange("p b n -> p (b n)")
        LN_BANK = (5, 7)
        V_BANK = (4, 5, 7)
        ctx_ps = dims(PS[:, 6, 0:HEADS * VW], HEADS, VW)

        in_patch, in_tokw, in_const, in_small = sem("in_patch"), sem("in_tokw"), sem("in_const"), sem("in_small")
        in_attn, in_abias, in_gate = sem2("in_attn"), sem2("in_abias"), sem2("in_gate")
        in_bias = sem("in_bias")
        in_shared, in_experts, in_last = sem("in_shared"), sem2("in_experts"), sem2("in_last")
        s_clear, s_psum0, s_zero = sem("s_clear"), sem("s_psum0"), sem("s_zero")
        s_braw, s_bsplit, s_bdram, s_bplace, s_sel = (sem(n) for n in ("s_braw", "s_bsplit", "s_bdram", "s_bplace", "s_sel"))
        s_dve = sem("dve_chain")
        s_embed, s_h0 = sem("s_embed"), sem("s_h0")
        s_ve = [sem(f"s_ve_{k}") for k in range(5)]
        s_rstd = [sem(f"s_rstd_{k}") for k in range(5)]
        s_xln = [sem(f"s_xln_{k}") for k in range(5)]
        s_tr = [sem(f"s_tr_{k}") for k in range(5)]
        s_xnT = [sem(f"s_xnT_{k}") for k in range(5)]
        s_qk, s_qkev, s_v, s_vev, s_vones, s_x3 = sem2("s_qk"), sem2("s_qkev"), sem2("s_v"), sem2("s_vev"), sem2("s_vones"), sem2("s_x3")
        s_scores, s_sadd, s_sub, s_exp = sem2("s_scores"), sem2("s_sadd"), sem2("s_sub"), sem2("s_exp")
        s_pt, s_ptev, s_pv, s_norm = sem2("s_pt"), sem2("s_ptev"), sem2("s_pv"), sem2("s_norm")
        s_ct, s_ctev, s_proj, s_res, s_hb = sem2("s_ct"), sem2("s_ctev"), sem2("s_proj"), sem2("s_res"), sem2("s_hb")
        s_logit, s_z, s_sig, s_mask, s_rank, s_pos, s_slots = (
            sem2(n) for n in ("s_logit", "s_z", "s_sig", "s_mask", "s_rank", "s_pos", "s_slots"))
        s_shup, s_shact, s_shdown, s_shev, s_hb2 = (sem(n) for n in ("s_shup", "s_shact", "s_shdown", "s_shev", "s_hb2"))
        s_scat = sem2("s_scat")
        s_xb = [sem2(f"s_xb{L}") for L in range(2)]
        s_ys = [sem2(f"s_ys{L}") for L in range(2)]
        s_xtr, s_xtev, s_up, s_silu, s_act = sem2("s_xtr"), sem2("s_xtev"), sem2("s_up"), sem2("s_silu"), sem2("s_act")
        s_atr, s_atev, s_down, s_yev = sem2("s_atr"), sem2("s_atev"), sem2("s_down"), sem2("s_yev")
        s_back = [[sem(f"s_back_{L}_{t}") for t in range(NT)] for L in range(2)]
        s_comb = sem2("s_comb")
        s_pad = sem("s_pad")
        s_out = sem("s_out")

        def block_steps(L, eng, first, step):
            first()
            step(0, 0, 0)
            step(1, 1, 1)
            turns = (ALWAYS - 2) // 2
            with eng.Fori(1, turns + 1) as i:
                step(i * 2, 0, 2)
                step(i * 2 + 1, 1, 3)
            for b in range(2 * turns + 2, ALWAYS):
                step(b, b % 2, b)
            eng.wait_ge(s_slots[L], 1)
            used = eng.value_load(be_i[0:1, BLOCKS_USED:BLOCKS_USED + 1], min_val=ALWAYS, max_val=BLOCKS[L])
            used_reg = eng.to_reg(used)
            for b in range(ALWAYS, BLOCKS[L]):
                with eng.If_cmp(used_reg, b, 'IS_GT'):
                    step(b, b % 2, b)

        block = ctx.enter_context(nc.Block())

        @block.sync
        def _(sp):
            for c in range(3):
                sp.dma_start(patch[:, 2 * c:2 * c + 2, :], a["patches"][:, 2 * c:2 * c + 2, :]).then_inc(in_patch, 16)
                sp.dma_start(tokw[:, 2 * c:2 * c + 2, :], a["tok_w"][:, 2 * c:2 * c + 2, :]).then_inc(in_tokw, 16)
            sp.dma_start(cst[:, :], a["consts"]).then_inc(in_const, 16)
            sp.dma_start(wA[:, 0:1024], a["wq0"]).then_inc(in_attn[0], 16)
            sp.dma_start(wA[:, 1024:1280], a["wk0"]).then_inc(in_attn[0], 16)
            sp.dma_start(wA[:, 2048:2176], a["wv0"]).then_inc(in_attn[0], 16)
            sp.dma_start(wA[:, 2560:3072], a["wo0"]).then_inc(in_attn[0], 16)
            sp.dma_start(bp, a["bp"].partition_broadcast(P)).then_inc(in_small, 16)
            sp.dma_start(sbd, a["sbd"].partition_broadcast(P)).then_inc(in_small, 16)
            sp.dma_start(sbu, a["sbu"]).then_inc(in_small, 16)
            sp.dma_start(gb, a["gamma_beta"]).then_inc(in_small, 16)
            sp.dma_start(braw, a["biases"]).then_inc(s_braw, 16)
            sp.dma_start(selraw, a["select"]).then_inc(s_braw, 16)
            sp.dma_start(gateT[:, :, 0:8], a["gate0"]).then_inc(in_gate[0], 16)
            sp.dma_start(gbias[:, 0:8], a["gbias0"].partition_broadcast(P)).then_inc(in_gate[0], 16)
            sp.wait_ge(s_clear, 1)
            for L in range(2):
                sp.dma_start(a["xs"][L].rearrange("(b p) d -> p b d", p=P),
                             zeros.unsqueeze(1).broadcast_to([P, BLOCKS[L], D])).then_inc(s_zero, 16)
                n = BLOCKS[L] - ALWAYS
                sp.dma_start(a["ys"][L].rearrange("(b p) d -> p b d", p=P)[:, ALWAYS:, :],
                             zeros.unsqueeze(1).broadcast_to([P, n, D])).then_inc(s_zero, 16)
            sp.wait_ge(s_bsplit, 3)
            for i in range(3):
                sp.dma_start(a["bias_parts"][i].rearrange("(p n) -> p n", p=P), bparts[i]).then_inc(s_bdram, 16)
            sp.dma_start(slot(0, 0, 4096), a["experts0"][0]).then_inc(in_shared, 16)
            for s in range(1, 7):
                sp.dma_start(slot(s, 0, 4096), a["experts0"][s]).then_inc(in_experts[0], 16)
            sp.wait_ge(s_bdram, 48)

            def place_biases(e0, e1):
                wb = W[:, :].bitcast(BF16)
                spare = dims(wb[0:9, :], 9, 2 * SLOT)
                for seg in range(3):
                    src = a["bias_parts"].rearrange("j (e s n) -> s j e n", e=8, s=3)[seg, :, e0:e1, :]
                    sp.dma_start(spare[3 * seg:3 * seg + 3, 1 + e0:1 + e1, 8192:8704], src).then_inc(in_bias, 16)

            place_biases(0, 6)
            sp.wait_ge(s_v[0], IMGS)
            sp.dma_start(abias, a["attn_bias0"]).then_inc(in_abias[0], 16)
            sp.wait_ge(s_proj[0], NT)
            for s in range(7, 9):
                sp.dma_start(slot(s, 0, 4096), a["experts0"][s]).then_inc(in_last[0], 16)
            place_biases(6, 8)
            sp.dma_start(wA[:, 0:1024], a["wq1"]).then_inc(in_attn[1], 16)
            sp.dma_start(wA[:, 1024:2048], a["wk1"]).then_inc(in_attn[1], 16)
            sp.dma_start(wA[:, 2048:2560], a["wv1"]).then_inc(in_attn[1], 16)
            sp.dma_start(wA[:, 2560:3072], a["wo1"]).then_inc(in_attn[1], 16)

            def rows(L):
                def load(b, par, k):
                    if k >= 2:
                        sp.wait_ge(s_xtr[L], b - 1)
                    sp.dma_start(xb[par], a["xs"][L][bass.ds(b * P, P), :]).then_inc(s_xb[L][par], 16)

                def step(b, par, k):
                    if k < BLOCKS[L] - 2:
                        load(b + 2, par, 2)
                    sp.wait_ge(s_yev[L], b + 1)
                    sp.dma_start(a["ys"][L][bass.ds(b * P, P), :], ys[par]).then_inc(s_ys[L][par], 16)

                def first():
                    sp.wait_ge(s_scat[L], 16 * 2 * NT)
                    load(0, 0, 0)
                    load(1, 1, 1)

                block_steps(L, sp, first, step)

            rows(0)
            sp.dma_start(gateT[:, :, :], a["gate1"]).then_inc(in_gate[1], 16)
            sp.dma_start(gbias[:, :], a["gbias1"].partition_broadcast(P)).then_inc(in_gate[1], 16)
            sp.wait_ge(s_v[1], IMGS)
            sp.dma_start(abias, a["attn_bias1"]).then_inc(in_abias[1], 16)
            sp.wait_ge(s_proj[1], NT)
            for s in range(7, 9):
                sp.dma_start(slot(s, 0, SLOT), a["experts1"][s]).then_inc(in_last[1], 16)
            rows(1)
            for t in range(NT):
                sp.wait_ge(s_comb[1], 2 * (t + 1))
                sp.dma_start(out[t * P:t * P + ROWS[t], :], h[0:ROWS[t], t, :]).then_inc(s_out, 16)
            sp.wait_ge(s_out, 16 * NT)

        @block.gpsimd
        def _(g):
            def power(k):
                g.wait_ge(s_ve[k], 1)
                nc.gpsimd.tensor_tensor(rstd, ve, mhalf, ALU.pow).then_inc(s_rstd[k], 1)

            def triple(L, k_ln):
                g.wait_ge(s_xnT[k_ln], NT)
                src = dims(xnT[:, 1, :], IMGS, PATCHES).unsqueeze(2).broadcast_to([P, IMGS, 3, PATCHES])
                nc.gpsimd.tensor_copy(x3[1], src).then_inc(s_x3[L], 1)

            def scatter(L, k_ln):
                g.wait_ge(s_zero, 64)
                g.wait_ge(s_pos[L], 2)
                for k in range(2):
                    for t in range(NT):
                        n = ROWS[t]
                        g.indirect_dma_start(
                            a["xs"][L], bass.IndirectOffsetOnAxis(pos_i[0:n, k, t:t + 1].bitcast(U32), 0),
                            xln[0:n, t, :], None).then_inc(s_scat[L], 16)

            def gather(L):
                used = g.value_load(be_i[0:1, BLOCKS_USED:BLOCKS_USED + 1], min_val=ALWAYS, max_val=BLOCKS[L])

                def through(b):
                    g.wait_ge(s_ys[L][b % 2], 16 * (b // 2 + 1))
                    g.wait_ge(s_act[L], 2 * min(b + 2, BLOCKS[L]))

                through(ALWAYS - 2)
                through(ALWAYS - 1)
                used_reg = g.to_reg(used)
                for b in range(ALWAYS, BLOCKS[L]):
                    with g.If_cmp(used_reg, b, 'IS_GT'):
                        through(b)
                for t in range(NT):
                    for k in range(2):
                        m = ROWS[t]
                        g.indirect_dma_start(
                            back[0:m, k, t, :], None, a["ys"][L],
                            bass.IndirectOffsetOnAxis(pos_i[0:m, k, t:t + 1].bitcast(U32), 0),
                        ).then_inc(s_back[L][t], 16)

            g.wait_ge(s_clear, 3)
            power(0)
            g.wait_ge(s_xln[0], NT)
            g.wait_ge(in_small, 64)
            nc.gpsimd.tensor_tensor(h, h, bp.unsqueeze(1).broadcast_to([P, NT, D]), ALU.add).then_inc(s_hb[0], 1)
            triple(0, 0)
            power(1)
            nc.gpsimd.tensor_scalar(sbd, sbd, 0.1, None, ALU.mult).then_inc(s_hb2, 1)
            g.wait_ge(s_hb2, 1)
            g.wait_ge(s_xln[1], NT)
            nc.gpsimd.tensor_tensor(h, h, sbd.unsqueeze(1).broadcast_to([P, NT, D]), ALU.add).then_inc(s_hb2, 1)
            scatter(0, 1)
            def load_expert(s):
                g.dma_start(slot(s, 0, SLOT), a["experts1"][s]).then_inc(in_experts[1], 16)

            g.wait_ge(s_shdown, NT)
            load_expert(0)
            g.wait_ge(s_down[0], NT)
            load_expert(1)
            g.wait_ge(s_slots[0], 1)
            gather(0)
            for s in range(2, 7):
                load_expert(s)
            power(2)
            power(3)
            g.wait_ge(s_xln[2], NT)
            nc.gpsimd.tensor_tensor(h, h, xln, ALU.add).then_inc(s_hb[1], 1)
            triple(1, 3)
            power(4)
            scatter(1, 4)
            g.wait_ge(s_slots[1], 1)
            gather(1)

        @block.tensor
        def _(pe):
            mm = nc.tensor.matmul

            def transposes_ln(k, src):
                for t in range(NT):
                    n = ROWS[t]
                    pe.wait_ge(s_xln[k], t + 1)
                    if t >= 2:
                        pe.wait_ge(s_xnT[k], t - 1)
                    for c in range(2):
                        last = nc.tensor.transpose(PS[:, LN_BANK[t % 2], c * P:c * P + n],
                                                   src[0:n, t, c * P:(c + 1) * P], ident[0:n, 0:n])
                    last.then_inc(s_tr[k], 1)

            def attention(L, k_ln):
                dq = DQ[L]
                pe.wait_ge(in_attn[L], 64)
                pe.wait_ge(s_xnT[k_ln], NT)
                items = [(wq, c, i) for c in range(4) for i in range(2)]
                items += [(wk[L], c, i) for c in range(KCHUNKS[L]) for i in range(2)]
                for i in range(IMGS + 4):
                    if i < len(items):
                        w, c, half = items[i]
                        if i >= 4:
                            pe.wait_ge(s_qkev[L], i - 3)
                        for k in range(2):
                            last = mm(PS[:, i % 4, 0:HALF], w[:, k, c * P:(c + 1) * P],
                                      xnT[:, k, half * HALF:(half + 1) * HALF], start=(k == 0), stop=(k == 1))
                        last.then_inc(s_qk[L], 1)
                    if i < 4:
                        continue
                    i -= 4
                    if i == 0:
                        pe.wait_ge(s_x3[L], 2)
                    if i >= 3:
                        pe.wait_ge(s_vev[L], i - 2)
                    for k in range(2):
                        last = mm(PS[0:108, V_BANK[i % 3], 0:VCOLS[L]],
                                  x3[k][:, i, :, :].rearrange("p r q -> p (r q)"), wv[L][:, k, :],
                                  start=(k == 0), stop=(k == 1))
                    last.then_inc(s_v[L], 1)

                def scores(p):
                    if p == 0:
                        pe.wait_ge(s_qkev[L], len(items))
                    else:
                        pe.wait_ge(s_sadd[L], p)
                    for par in range(2):
                        for c in range(4):
                            for j in range(4):
                                at = (2 * p + par) * PATCHES
                                col = c * PATCHES
                                last = mm(PS[64 * par:64 * par + PATCHES, j, col:col + PATCHES],
                                          qT[32 * j:32 * j + dq, c, at:at + PATCHES],
                                          kT[32 * j:32 * j + dq, c if L else 0, at:at + PATCHES],
                                          start=True, stop=True)
                    last.then_inc(s_scores[L], 1)

                def prob_turn(p):
                    pe.wait_ge(s_exp[L], p + 1)
                    if p >= 1:
                        pe.wait_ge(s_ptev[L], 2 * p)
                    else:
                        pe.wait_ge(s_vev[L], IMGS)
                    for g, (h0, nh) in enumerate(GROUPS):
                        last = nc.tensor.transpose(
                            ps_flat[0:nh * PATCHES, 4 * 512 + g * P:4 * 512 + (g + 1) * P],
                            prob[p % 2][:, h0 * PATCHES:(h0 + nh) * PATCHES], ident)
                    last.then_inc(s_pt[L], 1)

                def values(p):
                    pe.wait_ge(s_ptev[L], 2 * (p + 1))
                    if p >= 1:
                        pe.wait_ge(s_norm[L], p)
                    else:
                        pe.wait_ge(s_vones[L], 2)
                    for par in range(2):
                        for g, (h0, nh) in enumerate(GROUPS):
                            k = nh * PATCHES
                            last = mm(PS[64 * par:64 * par + PATCHES, 6, h0 * VW:(h0 + nh) * VW],
                                      pT[p % 2][0:k, g, par * PATCHES:(par + 1) * PATCHES],
                                      vblk[0:k, 2 * p + par, h0:h0 + nh, :], start=True, stop=True)
                    last.then_inc(s_pv[L], 1)

                def ctx_turn(p):
                    pe.wait_ge(s_norm[L], p + 1)
                    if p >= 1:
                        pe.wait_ge(s_ctev[L], p)
                    for c in range(2):
                        last = nc.tensor.transpose(PS[:, 7, c * P:(c + 1) * P],
                                                   ctxn[p % 2][:, c * P:(c + 1) * P], ident)
                    last.then_inc(s_ct[L], 1)

                for i in range(PAIRS + 2):
                    if i < PAIRS:
                        scores(i)
                    if 1 <= i <= PAIRS:
                        prob_turn(i - 1)
                    if i >= 2:
                        ctx_turn(i - 2)
                    if 1 <= i <= PAIRS:
                        values(i - 1)
                pe.wait_ge(s_ctev[L], PAIRS)
                for t in range(NT):
                    n = ROWS[t]
                    for k in range(2):
                        last = mm(PS[0:n, t, 0:D], ctxT[:, k, t * P:t * P + n], wo[:, k, :],
                                  start=(k == 0), stop=(k == 1))
                    last.then_inc(s_proj[L], 1)

            def logits(L, k_ln):
                pe.wait_ge(in_gate[L], 32)
                pe.wait_ge(s_xnT[k_ln], NT)
                for t in range(NT):
                    n = ROWS[t]
                    for k in range(2):
                        last = mm(PS[0:n, 7, 16 * t:16 * t + EXPERTS[L]], xnT[:, k, t * P:t * P + n],
                                  gateT[:, k, 0:EXPERTS[L]], start=(k == 0), stop=(k == 1))
                last.then_inc(s_logit[L], 1)

            def ranks(L):
                E = EXPERTS[L]
                M = dims(rt[:, 0:NT * E], NT, E)
                ones = one.broadcast_to([P, P])
                pe.wait_ge(s_mask[L], 1)
                for t in range(NT):
                    last = mm(PS[:, 6, 16 * t:16 * t + E], const("tri"), M[:, t, :], start=True, stop=(t == 0))
                    for u in range(t):
                        last = mm(PS[:, 6, 16 * t:16 * t + E], ones, M[:, u, :], start=False, stop=(u == t - 1))
                for t in range(NT):
                    last = mm(PS[:, 6, 80:80 + E], ones, M[:, t, :], start=(t == 0), stop=(t == NT - 1))
                last.then_inc(s_rank[L], 1)

            def shared_up():
                pe.wait_ge(in_shared, 16)
                for i in range(16):
                    c, half = i // 2, i % 2
                    if i >= 4:
                        pe.wait_ge(s_shact, i - 3)
                    for k in range(2):
                        last = mm(PS[:, i % 4, 0:HALF], slot(0, k * 1024 + c * P, P),
                                  xnT[:, k, half * HALF:(half + 1) * HALF], start=(k == 0), stop=(k == 1))
                    last.then_inc(s_shup, 1)

            def shared_down():
                pe.wait_ge(s_shact, 16)
                for t in range(NT):
                    n = ROWS[t]
                    if t >= 2:
                        pe.wait_ge(s_shev, t - 1)
                    for f in range(8):
                        last = mm(PS[0:n, 4 + t % 2, 0:D], shT[:, f, t * P:t * P + n],
                                  slot(0, 2048 + f * D, D), start=(f == 0), stop=(f == 7))
                    last.then_inc(s_shdown, 1)

            def experts(L):
                seg = SEG[L]
                wb = W[:, :].bitcast(BF16)

                def rows_turn(b, par, k):
                    pe.wait_ge(s_xb[L][par], (b // 2 + 1) * 16 if isinstance(b, int) else (b - par) * 8 + 16)
                    if k >= 1:
                        pe.wait_ge(s_xtev[L], b)
                    for c in range(2):
                        last = nc.tensor.transpose(PS[:, 7, c * P:(c + 1) * P],
                                                   xb[par][:, c * P:(c + 1) * P], ident)
                    last.then_inc(s_xtr[L], 1)

                def expert_of(b):
                    return pe.value_load(be_i[0:1, bass.ds(b, 1)], min_val=0, max_val=8)

                def up(b, par, k, s, e):
                    pe.wait_ge(s_xtev[L], b + 1)
                    if k >= 1:
                        pe.wait_ge(s_act[L], 2 * b + s - 1)
                    for part in range(L + 1):
                        bank = s + 2 * part
                        for c in range(2):
                            off = e * SLOT + part * 2 * HID[L] + c * HID[L] + s * seg
                            last = mm(PS[:, bank, 0:seg], xbT[par][:, c, :], W[:, bass.ds(off, seg)],
                                      start=(c == 0), stop=(L == 1 and c == 1))
                        if L == 0:
                            last = mm(PS[:, bank, 0:seg], sel[:, s, :], wb[0:9, bass.ds(e * 2 * SLOT + 8192, seg)],
                                      start=False, stop=True)
                    last.then_inc(s_up[L], 1)

                def act_turn(b, par, k):
                    pe.wait_ge(s_act[L], 2 * b + 2)
                    if k >= 1:
                        pe.wait_ge(s_atev[L], 2 * b)
                    elif L == 0:
                        pe.wait_ge(s_shev, NT)
                    for f in range(FCH[L]):
                        last = nc.tensor.transpose(ps_flat[:, 4 * 512 + f * P:4 * 512 + (f + 1) * P],
                                                   act[par][:, f * P:(f + 1) * P], ident)
                        if f in (3, FCH[L] - 1):
                            last.then_inc(s_atr[L], 1)

                def down(b, par, k, e):
                    pe.wait_ge(s_atev[L], 2 * b + 2)
                    if k >= 1:
                        pe.wait_ge(s_yev[L], b)
                    base = 2 * HID[L] * (L + 1)
                    y = PS[:, 6, 0:D]
                    for f in range(FCH[L]):
                        last = mm(y, actT[:, f * P:(f + 1) * P], W[:, bass.ds(e * SLOT + base + f * D, D)],
                                  start=(f == 0), stop=(L == 1 and f == FCH[L] - 1))
                    if L == 0:
                        last = mm(y, sel[:, 2, :], wb[0:9, bass.ds(e * 2 * SLOT + 8192, D)], start=False, stop=True)
                    last.then_inc(s_down[L], 1)

                def step(b, par, k):
                    more = k < BLOCKS[L] - 1
                    if more:
                        e1 = expert_of(b + 1)
                        up(b + 1, 1 - par, 1, 0, e1)
                    act_turn(b, par, k)
                    if more:
                        up(b + 1, 1 - par, 1, 1, e1)
                    if k < BLOCKS[L] - 2:
                        rows_turn(b + 2, par, 2)
                    down(b, par, k, expert_of(b))
                    if k >= ALWAYS - 1:
                        pe.wait_ge(s_xtev[L], min(b + 3, BLOCKS[L]))

                def first():
                    pe.wait_ge(s_slots[L], 1)
                    rows_turn(0, 0, 0)
                    rows_turn(1, 1, 1)
                    pe.wait_ge(in_experts[L], 16 * (6 + L))
                    pe.wait_ge(in_last[L], 32)
                    if L == 0:
                        pe.wait_ge(in_bias, 16 * 6)
                        pe.wait_ge(s_sel, 1)
                    e0 = expert_of(0)
                    up(0, 0, 0, 0, e0)
                    up(0, 0, 0, 1, e0)

                block_steps(L, pe, first, step)

            pe.wait_ge(s_psum0, 1)
            pe.wait_ge(in_patch, 48)
            pe.wait_ge(in_tokw, 48)
            for t in range(NT):
                n = ROWS[t]
                for k in range(6):
                    last = mm(PS[0:n, t, 0:D], patch[:, k, t * P:t * P + n], tokw[:, k, :],
                              start=(k == 0), stop=(k == 5))
                last.then_inc(s_embed, 1)
            pe.wait_ge(in_const, 16)
            transposes_ln(0, xln)
            attention(0, 0)
            transposes_ln(1, xln)
            logits(0, 1)
            shared_up()
            ranks(0)
            shared_down()
            experts(0)
            transposes_ln(3, xln2)
            attention(1, 3)
            transposes_ln(4, xln)
            logits(1, 4)
            ranks(1)
            experts(1)

        @block.scalar
        def _(ac):
            def copies_ln(k, affine=False):
                for t in range(NT):
                    n = ROWS[t]
                    ac.wait_ge(s_tr[k], t + 1)
                    src = dims(PS[:, LN_BANK[t % 2], 0:256], 2, P)[:, :, 0:n]
                    if not affine:
                        nc.scalar.copy(xnT[:, :, t * P:t * P + n], src).then_inc(s_xnT[k], 1)
                        continue
                    nc.scalar.activation(xnT[:, 0, t * P:t * P + n], src[:, 0, :], ACT.Identity,
                                         bias=gb[:, 2:3], scale=gb[:, 0:1])
                    nc.scalar.activation(xnT[:, 1, t * P:t * P + n], src[:, 1, :], ACT.Identity,
                                         bias=gb[:, 3:4], scale=gb[:, 1:2]).then_inc(s_xnT[k], 1)

            def attention(L):
                n = 8 + 2 * KCHUNKS[L]
                for i in range(n):
                    ac.wait_ge(s_qk[L], i + 1)
                    half = i % 2
                    if i < 8:
                        nc.scalar.mul(qT[:, i // 2, half * HALF:(half + 1) * HALF], PS[:, i % 4, 0:HALF],
                                      QSCALE[L]).then_inc(s_qkev[L], 1)
                    else:
                        if L == 0 and i == 8:
                            ac.wait_ge(s_bdram, 48)
                            ac.wait_ge(s_sel, 1)
                        nc.scalar.copy(kT[:, (i - 8) // 2, half * HALF:(half + 1) * HALF],
                                       PS[:, i % 4, 0:HALF]).then_inc(s_qkev[L], 1)
                for i in range(PAIRS + 2):
                    if i < PAIRS:
                        ac.wait_ge(s_sub[L], i + 1)
                        nc.scalar.activation(prob[i % 2], prob[i % 2], ACT.Exp).then_inc(s_exp[L], 1)
                    if 1 <= i <= PAIRS:
                        p = i - 1
                        ac.wait_ge(s_pt[L], p + 1)
                        if p >= 2:
                            ac.wait_ge(s_pv[L], p - 1)
                        src = dims(ps_flat[:, 4 * 512:4 * 512 + 6 * P], 6, 2, 64)
                        for g0, g1, k in ((0, 5, 108), (5, 6, PATCHES)):
                            dst = pT[p % 2][0:k, g0:g1, :].rearrange("p g (i q) -> p g i q", i=2)
                            nc.scalar.copy(dst, src[0:k, g0:g1, :, 0:PATCHES]).then_inc(s_ptev[L], 1)
                    if i >= 2:
                        p = i - 2
                        ac.wait_ge(s_ct[L], p + 1)
                        src = dims(PS[:, 7, 0:256], 2, 2, 64)[:, :, :, 0:PATCHES]
                        dst = ctxT[:, :, 72 * p:72 * (p + 1)].rearrange("p c (i q) -> p c i q", i=2)
                        nc.scalar.copy(dst, src).then_inc(s_ctev[L], 1)

            def sigmoid(L):
                E = EXPERTS[L]
                ac.wait_ge(s_z[L], 1)
                nc.scalar.activation(rt[:, 2 * 45:2 * 45 + NT * E], rt[:, 45:45 + NT * E],
                                     ACT.Sigmoid).then_inc(s_sig[L], 1)

            def experts(L):
                seg = SEG[L]

                def rows_copy(b, par, k):
                    ac.wait_ge(s_xtr[L], b + 1)
                    if k >= 2:
                        ac.wait_ge(s_up[L], 2 * b - 2)
                    nc.scalar.copy(xbT[par], dims(PS[:, 7, 0:256], 2, P)
                                   ).then_inc(s_xtev[L], 1)

                def gate(b, par, k, s):
                    ac.wait_ge(s_up[L], 2 * b + s + 1)
                    if k >= 2:
                        ac.wait_ge(s_atr[L], 2 * b - 2)
                    nc.scalar.activation(act[par][:, s * seg:(s + 1) * seg], PS[:, s, 0:seg],
                                         ACT.Silu if L else ACT.Gelu).then_inc((s_silu if L else s_act)[L], 1)

                def step(b, par, k):
                    if k < BLOCKS[L] - 1:
                        gate(b + 1, 1 - par, k + 1, 0)
                        gate(b + 1, 1 - par, k + 1, 1)
                    if k < BLOCKS[L] - 2:
                        rows_copy(b + 2, par, 2)

                def first():
                    rows_copy(0, 0, 0)
                    rows_copy(1, 1, 1)
                    if L == 1:
                        ac.wait_ge(s_pad, 1)
                    gate(0, 0, 0, 0)
                    gate(0, 0, 0, 1)

                block_steps(L, ac, first, step)

            copies_ln(0)
            attention(0)
            copies_ln(1)
            sigmoid(0)
            ac.wait_ge(in_small, 64)
            for i in range(16):
                c, half = i // 2, i % 2
                ac.wait_ge(s_shup, i + 1)
                nc.scalar.activation(shT[:, c, half * HALF:(half + 1) * HALF], PS[:, i % 4, 0:HALF],
                                     ACT.Gelu, bias=sbu[:, c:c + 1]).then_inc(s_shact, 1)
            experts(0)
            copies_ln(3, affine=True)
            attention(1)
            copies_ln(4)
            sigmoid(1)
            experts(1)

        @block.vector
        def _(v):
            chained = [0]

            def link(ins):
                chained[0] += 1
                ins.then_inc(s_dve, 1)
                v.wait_ge(s_dve, chained[0])

            TT, TS, STT = nc.vector.tensor_tensor, nc.vector.tensor_scalar, nc.vector.scalar_tensor_tensor

            def layernorm(k, src, dst):
                for t in range(NT):
                    last = nc.vector.bn_stats(stats[:, t, :], src[:, t, :])
                link(last)
                for t in range(NT):
                    last = nc.vector.bn_aggr(mv[:, t, :], stats[:, t, :])
                link(last)
                TS(ve, mv[:, :, 1], EPS_LN, None, ALU.add).then_inc(s_ve[k], 1)
                v.wait_ge(s_rstd[k], 1)
                for t in range(NT):
                    TS(dst[:, t, :], src[:, t, :], mv[:, t, 0:1], rstd[:, t:t + 1], ALU.subtract,
                       ALU.mult).then_inc(s_xln[k], 1)

            def attention(L, k_ln):
                mask = const("vmask")[0:108, :]
                v.wait_ge(s_xnT[k_ln], NT)
                nc.vector.tensor_copy(x3[0], dims(xnT[:, 0, :], IMGS, PATCHES).unsqueeze(2).broadcast_to(
                    [P, IMGS, 3, PATCHES])).then_inc(s_x3[L], 1)
                nc.vector.tensor_copy(vblk[0:108, :, :, DH],
                                      mask.unsqueeze(1).broadcast_to([108, IMGS, HEADS])).then_inc(s_vones[L], 1)
                nc.vector.memset(PS[:, 6, 0:HEADS * VW], 1.0).then_inc(s_vones[L], 1)
                for i in range(IMGS):
                    v.wait_ge(s_v[L], i + 1)
                    if L == 0:
                        dst = vblk[0:108, i, :, 0:DH].rearrange("p (j c) d -> p j c d", j=4)
                        src = dims(PS[0:108, V_BANK[i % 3], 0:64], 4, DH).unsqueeze(2).broadcast_to([108, 4, 4, DH])
                        m = dims(mask, 4, 4).unsqueeze(3).broadcast_to([108, 4, 4, DH])
                    else:
                        dst = vblk[0:108, i, :, 0:DH]
                        src = dims(PS[0:108, V_BANK[i % 3], 0:256], HEADS, DH)
                        m = mask.unsqueeze(2).broadcast_to([108, HEADS, DH])
                    TT(dst, src, m, ALU.mult).then_inc(s_vev[L], 1)
                v.wait_ge(in_abias[L], 16)

                def softmax(p):
                    t = prob[p % 2]
                    v.wait_ge(s_scores[L], p + 1)
                    if p >= 2:
                        v.wait_ge(s_pt[L], p - 1)
                    TT(dims(t, 4, 144), PS[:, 0:4, 0:144], dims(abias, 4, 144), ALU.add).then_inc(s_sadd[L], 1)
                    v.wait_ge(s_sadd[L], p + 1)
                    link(nc.vector.tensor_reduce(nmax, dims(t, HEADS, PATCHES), AX, ALU.max))
                    TT(dims(t, HEADS, PATCHES), dims(t, HEADS, PATCHES),
                       nmax.unsqueeze(2).broadcast_to([P, HEADS, PATCHES]), ALU.subtract).then_inc(s_sub[L], 1)

                def normalize(p):
                    v.wait_ge(s_pv[L], p + 1)
                    link(nc.vector.reciprocal(rinv, ctx_ps[:, :, DH]))
                    if p >= 2:
                        v.wait_ge(s_ct[L], p - 1)
                    elif L == 0:
                        v.wait_ge(s_zero, 64)
                    TT(dims(ctxn[p % 2], HEADS, DH), ctx_ps[:, :, 0:DH],
                       rinv.unsqueeze(2).broadcast_to([P, HEADS, DH]), ALU.mult).then_inc(s_norm[L], 1)

                for i in range(PAIRS + 1):
                    if i < PAIRS:
                        softmax(i)
                    if i >= 1:
                        normalize(i - 1)
                v.wait_ge(s_hb[L], 1)
                for t in range(NT):
                    n = ROWS[t]
                    v.wait_ge(s_proj[L], t + 1)
                    last = TT(h[0:n, t, :], PS[0:n, t, 0:D], h[0:n, t, :], ALU.add)
                link(last)

            def route(L):
                E = EXPERTS[L]

                def tmp(i):
                    return dims(rt[:, 45 * i:45 * i + NT * E], NT, E)

                M, z, sig, key, oh1, oh2, t1, t2 = (tmp(i) for i in range(8))
                r5 = [rt[:, 360 + 5 * i:365 + 5 * i] for i in range(8)]
                nb, cum, start = (rt[:, 400 + 9 * i:400 + 9 * i + E] for i in range(3))
                ids = const("ids")[:, 0:E].unsqueeze(1).broadcast_to([P, NT, E])

                def bc(x):
                    return x.unsqueeze(2).broadcast_to([P, NT, E])

                v.wait_ge(s_logit[L], 1)
                TT(z, dims(PS[:, 7, 0:80], NT, 16)[:, :, 0:E], gbias[:, 0:E].unsqueeze(1).broadcast_to([P, NT, E]),
                   ALU.add).then_inc(s_z[L], 1)
                v.wait_ge(s_z[L], 1)
                link(TS(key, z, 17.0, -103.0, ALU.min, ALU.max))
                for oh, m, i in ((oh1, r5[0], r5[1]), (oh2, r5[2], r5[3])):
                    link(nc.vector.tensor_reduce(m, key, AX, ALU.max))
                    link(TT(t1, key, bc(m), ALU.is_equal))
                    link(STT(t1, t1, -99.0, ids, ALU.mult, ALU.add))
                    link(nc.vector.tensor_reduce(i, t1, AX, ALU.min))
                    link(TS(i, i, 99.0, None, ALU.add))
                    link(TT(oh, ids, bc(i), ALU.is_equal))
                    if oh is oh1:
                        link(STT(key, oh1, -1e6, key, ALU.mult, ALU.add))
                link(TT(M, oh1, oh2, ALU.add))
                TT(M, M, bc(const("valid")), ALU.mult).then_inc(s_mask[L], 1)
                v.wait_ge(s_sig[L], 1)
                TT(t1, sig, oh1, ALU.mult)
                link(TT(t2, sig, oh2, ALU.mult))
                nc.vector.tensor_reduce(r5[0], t1, AX, ALU.add)
                link(nc.vector.tensor_reduce(r5[1], t2, AX, ALU.add))
                link(STT(r5[2], r5[0], EPS_TOPK[L], r5[1], ALU.add, ALU.add))
                link(nc.vector.reciprocal(r5[3], r5[2]))
                TT(pw[:, 0, :], r5[0], r5[3], ALU.mult)
                link(TT(pw[:, 1, :], r5[1], r5[3], ALU.mult))
                v.wait_ge(s_rank[L], 1)
                c5 = dims(rt[:, 45:45 + NT * E], E, NT)
                link(TT(c5, PS[:, 6, 80:80 + E].unsqueeze(2).broadcast_to([P, E, NT]),
                        const("thr").unsqueeze(1).broadcast_to([P, E, NT]), ALU.is_gt))
                link(nc.vector.tensor_reduce(nb, c5, AX, ALU.add))
                ee = dims(rt[:, 90:90 + E * E], E, E)
                link(TT(ee, nb.unsqueeze(1).broadcast_to([P, E, E]), dims(const(f"le{L}"), E, E), ALU.mult))
                link(nc.vector.tensor_reduce(cum, ee, AX, ALU.add))
                link(TT(start, cum, nb, ALU.subtract))
                link(TS(start, start, float(P), None, ALU.mult))
                place = tmp(1)
                link(TT(place, dims(PS[:, 6, 0:80], NT, 16)[:, :, 0:E],
                        start.unsqueeze(1).broadcast_to([P, NT, E]), ALU.add))
                TT(t1, place, oh1, ALU.mult)
                link(TT(t2, place, oh2, ALU.mult))
                nc.vector.tensor_reduce(r5[4], t1, AX, ALU.add)
                link(nc.vector.tensor_reduce(r5[5], t2, AX, ALU.add))
                nc.vector.tensor_copy(pos_i[:, 0, :], r5[4]).then_inc(s_pos[L], 1)
                nc.vector.tensor_copy(pos_i[:, 1, :], r5[5]).then_inc(s_pos[L], 1)
                nb_, c1 = BLOCKS[L], rt[0:1, 90:90 + BLOCKS[L] * E]
                c1 = dims(c1, nb_, E)
                link(TT(c1, cum[0:1, :].unsqueeze(1).broadcast_to([1, nb_, E]),
                        const("blk")[0:1, 0:nb_].unsqueeze(2).broadcast_to([1, nb_, E]), ALU.is_le))
                bf = rt[0:1, 260:260 + nb_]
                link(nc.vector.tensor_reduce(bf, c1, AX, ALU.add))
                nc.vector.tensor_copy(be_i[:, BLOCKS_USED:BLOCKS_USED + 1], cum[0:1, E - 1:E])
                TS(be_i[:, 0:nb_], bf, float(E - 1), float(FIRST_SLOT[L]), ALU.min, ALU.add).then_inc(s_slots[L], 1)

            def experts(L):
                seg = SEG[L]

                def hidden(b, par, k, s):
                    v.wait_ge(s_silu[L], 2 * b + s + 1)
                    part = act[par][:, s * seg:(s + 1) * seg]
                    TT(part, part, PS[:, 2 + s, 0:seg], ALU.mult).then_inc(s_act[L], 1)

                def turned(b, par, k, half):
                    v.wait_ge(s_atr[L], 2 * b + half + 1)
                    if k >= 1:
                        v.wait_ge(s_down[L], b)
                    n = 512 if half == 0 else FCH[L] * P - 512
                    nc.vector.tensor_copy(actT[:, half * 512:half * 512 + n],
                                          PS[:, 4 + half, 0:n]).then_inc(s_atev[L], 1)

                def step(b, par, k):
                    if L == 1 and k < BLOCKS[L] - 1:
                        hidden(b + 1, 1 - par, k + 1, 0)
                    turned(b, par, k, 0)
                    turned(b, par, k, 1)
                    if L == 1 and k < BLOCKS[L] - 1:
                        hidden(b + 1, 1 - par, k + 1, 1)
                    v.wait_ge(s_down[L], b + 1)
                    if k >= 2:
                        v.wait_ge(s_ys[L][par], (b // 2) * 16 if isinstance(b, int) else (b - par) * 8)
                    nc.vector.tensor_copy(ys[par], PS[:, 6, 0:D]).then_inc(s_yev[L], 1)

                def first():
                    if L == 1:
                        hidden(0, 0, 0, 0)
                        hidden(0, 0, 0, 1)

                block_steps(L, v, first, step)

            def combine(L):
                for t in range(NT):
                    n = ROWS[t]
                    v.wait_ge(s_back[L][t], 32)
                    for k in range(2):
                        STT(h[0:n, t, :], back[0:n, k, t, :], pw[0:n, k, t:t + 1], h[0:n, t, :],
                            ALU.mult, ALU.add).then_inc(s_comb[L], 1)
                        v.wait_ge(s_comb[L], 2 * t + k + 1)

            nc.vector.memset(zeros, 0.0).then_inc(s_clear, 1)
            nc.vector.memset(h[64:P, NT - 1, :], 0.0).then_inc(s_clear, 1)
            nc.vector.memset(mhalf, -0.5).then_inc(s_clear, 1)
            nc.vector.memset(PS[:, :, :], 0.0).then_inc(s_psum0, 1)
            link(nc.vector.memset(one, 1.0))
            v.wait_ge(s_braw, 32)
            link(nc.vector.tensor_copy(bparts[0], braw))
            link(TT(brest, braw, bparts[0], ALU.subtract))
            link(nc.vector.tensor_copy(bparts[1], brest))
            link(TT(brest, brest, bparts[1], ALU.subtract))
            nc.vector.tensor_copy(bparts[2], brest).then_inc(s_bsplit, 3)
            nc.vector.tensor_copy(sel[:, :, :], selraw).then_inc(s_sel, 1)
            for t in range(NT):
                n = ROWS[t]
                v.wait_ge(s_embed, t + 1)
                last = nc.vector.tensor_copy(h[0:n, t, :], PS[0:n, t, 0:D])
            link(last)
            layernorm(0, h, xln)
            v.wait_ge(in_const, 16)
            attention(0, 0)
            layernorm(1, h, xln)
            route(0)
            v.wait_ge(s_hb2, 2)
            for t in range(NT):
                n = ROWS[t]
                v.wait_ge(s_shdown, t + 1)
                last = STT(h[0:n, t, :], PS[0:n, 4 + t % 2, 0:D], 0.1, h[0:n, t, :], ALU.mult, ALU.add)
                last.then_inc(s_shev, 1)
            v.wait_ge(s_shev, NT)
            experts(0)
            combine(0)
            layernorm(2, h, xln)
            v.wait_ge(s_xln[2], NT)
            layernorm(3, xln, xln2)
            attention(1, 3)
            layernorm(4, h, xln)
            for i in range(2):
                last = nc.vector.memset(act[i][:, HID[1]:FCH[1] * P], 0.0)
            last.then_inc(s_pad, 1)
            route(1)
            experts(1)
            combine(1)


def host_layout(x):
    import numpy as np

    def g(name):
        return np.asarray(x[name])

    def kp(w):
        return w.reshape(-1, P, w.shape[1]).transpose(1, 0, 2)

    def flat(w):
        return w.reshape(P, -1)

    def heads4(w, dq):
        n = w.shape[1] // dq
        out = np.zeros((w.shape[0], n, 32), w.dtype)
        out[:, :, :dq] = w.reshape(w.shape[0], n, dq)
        return out.reshape(w.shape[0], n * 32)

    perm = np.array([4 * c + j for j in range(4) for c in range(4)])

    def perm_cols(w):
        return w.reshape(w.shape[0], HEADS, DH)[:, perm].reshape(w.shape[0], D)

    o = {}
    img = g("x").reshape(IMGS, 3, 6, 16, 6, 16).transpose(0, 1, 3, 5, 2, 4)
    patches = img.reshape(IMGS, PATCHES, FEAT).transpose(2, 0, 1).reshape(FEAT, TOK)
    o["patches"] = kp(patches)
    o["tok_w"] = kp(g("L0_tok_W"))
    o["wq0"] = flat(kp(heads4(g("L0_attn_Wq"), 8)))
    o["wk0"] = flat(kp(heads4(g("L0_attn_Wk"), 8)))
    o["wv0"] = flat(kp(g("L0_attn_Wv")))
    o["wo0"] = flat(kp(perm_cols(g("L0_attn_Wp").T).T))
    o["bp"], o["sbd"] = g("L0_attn_bp"), g("L0_ffn_sbd")
    o["sbu"] = g("L0_ffn_sbu").reshape(8, P).T
    o["wq1"] = flat(kp(heads4(g("L1_attn_Wq").T, 16)))
    o["wk1"] = flat(kp(heads4(g("L1_attn_Wk").T, 16)))
    o["wv1"] = flat(kp(perm_cols(g("L1_attn_Wv").T)))
    o["wo1"] = flat(kp(perm_cols(g("L1_attn_Wo")).T))
    o["gamma_beta"] = np.concatenate([g("L1_attn_ln_gamma").reshape(2, P).T, g("L1_attn_ln_beta").reshape(2, P).T], 1)
    o["gate0"] = kp(g("L0_ffn_gate_w").T)
    o["gbias0"] = g("L0_ffn_gate_bias")
    o["gate1"] = kp(np.concatenate([g("L1_ffn_gate_weight"), g("L1_ffn_new_gate_weight")]).T)
    o["gbias1"] = np.concatenate([np.zeros(8, np.float32), g("L1_ffn_gate_bias")])
    b = np.zeros((8, 1536), np.float32)
    b[:, :1024], b[:, 1024:1280] = g("L0_ffn_bu"), g("L0_ffn_bd")
    o["biases"] = b.reshape(P, 96)

    up0 = np.concatenate([g("L0_ffn_sWu")[None], g("L0_ffn_Wu")])
    dn0 = np.concatenate([g("L0_ffn_sWd")[None], g("L0_ffn_Wd")])
    o["experts0"] = np.stack([np.concatenate([flat(kp(up0[e].T)), flat(kp(dn0[e].T))], 1) for e in range(9)])
    w1 = np.concatenate([g("L1_ffn_w1"), g("L1_ffn_new_w1")])
    w2 = np.concatenate([g("L1_ffn_w2"), g("L1_ffn_new_w2")])
    w3 = np.concatenate([g("L1_ffn_w3"), g("L1_ffn_new_w3")])
    w2t = np.zeros((9, FCH[1] * P, D), np.float32)
    w2t[:, :HID[1]] = w2.transpose(0, 2, 1)
    o["experts1"] = np.stack([np.concatenate([flat(kp(w1[e].T)), flat(kp(w3[e].T)), flat(kp(w2t[e]))], 1)
                              for e in range(9)])

    i, j = np.arange(PATCHES)[:, None], np.arange(PATCHES)[None, :]
    causal = j > i
    slopes = (2.0 ** (-8.0 * np.arange(1, HEADS + 1) / HEADS)).astype(np.float32)
    alibi = (slopes[:, None, None] * (j - i).astype(np.float32) / np.float32(np.sqrt(8.0))).astype(np.float32)
    rel = g("L1_attn_rel")[:, np.clip(i - j, 0, 128)]
    for L, table in enumerate((alibi, rel)):
        slots = np.zeros((P, HEADS, PATCHES), np.float32)
        t = np.where(causal[None], np.float32(NEG), table)[perm].transpose(1, 0, 2)
        slots[0:PATCHES], slots[64:64 + PATCHES] = t, t
        o[f"attn_bias{L}"] = slots.reshape(P, -1)

    c = np.zeros((P, NCONST), np.float32)

    def put(name, value):
        at, n = CONST[name]
        c[:, at:at + n] = value

    put("ident", np.eye(P))
    put("tri", np.triu(np.ones((P, P)), 1))
    r = np.arange(P)
    put("vmask", (r[:, None] // PATCHES) == (np.arange(HEADS)[None] % 3))
    put("le0", np.tril(np.ones((8, 8))).reshape(1, -1))
    put("le1", np.tril(np.ones((9, 9))).reshape(1, -1))
    put("thr", P * np.arange(NT)[None])
    put("valid", (r[:, None] + P * np.arange(NT)[None]) < TOK)
    put("ids", np.arange(9)[None])
    put("blk", np.arange(18)[None])
    o["consts"] = c
    s = np.zeros((9, 3, P), np.float32)
    for k in range(9):
        s[k, k // 3] = 1
    o["select"] = s
    return {k: np.ascontiguousarray(w) for k, w in o.items()}


def kernel(**inputs):
    import concourse.bacc as bacc
    from concourse.bass_utils import run_bass_kernel_spmd as run

    nc = bacc.Bacc("TRN2", target_bir_lowering=False, num_devices=1)
    arrays = {f"in_{k}": w for k, w in host_layout(inputs).items()}
    a = {k[3:]: nc.dram_tensor(k, w.shape, F32, kind="ExternalInput").ap() for k, w in arrays.items()}
    a["xs"] = [nc.dram_tensor(f"sorted_rows_{L}", (BLOCKS[L] * P, D), F32, kind="Internal").ap() for L in range(2)]
    a["ys"] = [nc.dram_tensor(f"expert_rows_{L}", (BLOCKS[L] * P, D), F32, kind="Internal").ap() for L in range(2)]
    a["bias_parts"] = nc.dram_tensor("bias_parts", (3, 8 * 1536), BF16, kind="Internal").ap()
    out = nc.dram_tensor("out", (TOK, D), F32, kind="ExternalOutput").ap()
    tower(nc, a, out)
    r = run(nc, [arrays], core_ids=[0])
    return r.results[0]["out"].reshape(IMGS, PATCHES, D)
```

```python
from contextlib import ExitStack

import concourse.bass as bass
from concourse import mybir

F32 = mybir.dt.float32
BF16 = mybir.dt.bfloat16
I32 = mybir.dt.int32
U32 = mybir.dt.uint32
ACT = mybir.ActivationFunctionType
ALU = mybir.AluOpType
AX = mybir.AxisListType.X

P = 128
IMGS, PATCHES, D, FEAT = 16, 36, 256, 768
TOK = IMGS * PATCHES
NT = -(-TOK // P)
ROWS = [min(P, TOK - t * P) for t in range(NT)]
HALF = TOK // 2
PAIRS = IMGS // 2
HEADS, DH = 16, 16
DQ = (8, 16)
CH = (1, 2)
HB = 8
VCOLS = (64, 256)
QSCALE = (8.0 ** -0.5, 16.0 ** -0.5)
GROUPS = [(3 * g, min(3, HEADS - 3 * g)) for g in range(-(-HEADS // 3))]
VW = DH + 1
EPS_LN = 1e-5
EXPERTS = (8, 9)
HID = (1024, 704)
FCH = (8, 6)
SEG = (512, 352)
BLOCKS = tuple((2 * TOK + e * (P - 1)) // P for e in EXPERTS)
ALWAYS = -(-2 * TOK // P)
BLOCKS_USED = 18
SLOT = 4352
EPS_TOPK = (1e-6, 1e-20)
FIRST_SLOT = (1, 0)
NEG = -1e30

CONST = {}
_at = 0
for _name, _n in (("ident", P), ("tri", P), ("vmask", HEADS), ("kmask0", HEADS), ("kmask1", HEADS), ("le0", 64), ("le1", 81), ("thr", NT),
                  ("valid", NT), ("ids", 9), ("blk", 18)):
    CONST[_name] = (_at, _n)
    _at += _n
NCONST = _at


def dims(ap, *shape):
    names = "abcd"[:len(shape)]
    return ap.rearrange(f"p ({' '.join(names)}) -> p {' '.join(names)}", **dict(zip(names, shape)))


def tower(nc, a, out):
    ctx = ExitStack()
    with ctx:
        def sb(name, shape, dt=F32):
            return ctx.enter_context(nc.sbuf_tensor(name, shape, dt))

        def sem(name):
            return ctx.enter_context(nc.semaphore(name))

        def sem2(name):
            return [sem(f"{name}_{n}") for n in range(2)]

        W = sb("expert_slots", [P, 9 * SLOT])
        R1 = sb("phase_buffers", [P, 4864])
        R2 = sb("row_buffers", [P, 1024])
        wA = sb("attn_weights", [P, 2048])
        abias = sb("attn_bias", [P, HEADS * PATCHES])
        tri_b = sb("tri_bf16", [P, P], BF16)
        ones_b = sb("ones_bf16", [P, P], BF16)
        mask_b = sb("expert_mask", [P, NT + 1, 9], BF16)
        h_t = sb("h", [P, NT * D])
        x_t = sb("xln", [P, NT * D])
        xnT_t = sb("xnT", [P, 2 * TOK])
        cst = sb("consts", [P, NCONST])
        sel = sb("bias_select", [9, 3, P], BF16)
        small = sb("small", [P, 100])
        rt = sb("route", [P, 10 * 45])
        pos_i = sb("positions", [P, 2, NT], I32)
        be_i = sb("block_slots", [1, BLOCKS_USED + 1], I32)
        pw = sb("pair_weights", [P, 2, NT])
        gateT = sb("gateT", [P, 2, 9])
        gbias = sb("gate_bias", [P, 9])

        h = dims(h_t[:, :], NT, D)
        xln = dims(x_t[:, :], NT, D)
        xnT = dims(xnT_t[:, :], 2, TOK)

        def slot(s, off, n):
            return W[:, s * SLOT + off:s * SLOT + off + n]

        def const(name):
            o, n = CONST[name]
            return cst[:, o:o + n]

        ident = const("ident")
        vblk = dims(slot(7, 0, IMGS * HEADS * VW), IMGS, HEADS, VW)
        qT = dims(slot(8, 0, 2 * TOK), 2, TOK)
        kb = [dims(slot(8, 1152 + 1152 * i, 1152), 2, 2, HB * PATCHES) for i in range(2)]
        pT = [dims(slot(8, 3456 + 432 * i, 432), 6, 72) for i in range(2)]
        kT = dims(R1[:, 0:2 * TOK], 2, TOK)
        xln2 = dims(R1[:, 0:NT * D], NT, D)
        x3 = [dims(t, IMGS, 3, PATCHES) for t in (R1[:, 1152:1152 + 3 * TOK], R1[:, 2880:2880 + 3 * TOK])]
        ctxT = dims(R1[:, 2304:2304 + 2 * TOK], 2, TOK)
        prob = [R1[:, 3456 + 576 * i:3456 + 576 * (i + 1)] for i in range(2)]
        ctxn = [R2[:, 256 * i:256 * (i + 1)] for i in range(2)]
        zeros = R2[:, 0:256]
        bp = R2[:, 768:1024]
        wq = [dims(wA[:, 0:256], 2, 128), dims(wA[:, 0:512], 2, 256)]
        wk = [dims(wA[:, 512:768], 2, 128), dims(wA[:, 512:1024], 2, 256)]
        wv = [dims(wA[:, 1024:1152], 2, 64), dims(wA[:, 1024:1536], 2, 256)]
        wo = dims(wA[:, 1536:2048], 2, 256)
        patch = dims(slot(7, 0, 6 * TOK), 6, TOK)
        tokw = dims(slot(8, 0, 6 * D), 6, D)
        shT = dims(R1[:, 0:8 * TOK], 8, TOK)
        sbd = R1[:, 4608:4864]
        act = [R1[:, 1024 * i:1024 * (i + 1)] for i in range(2)]
        actT = R1[:, 2048:3072]
        ys = [R1[:, 3072 + 256 * i:3072 + 256 * (i + 1)] for i in range(2)]
        back = dims(R1[:, 0:2 * NT * D], 2, NT, D)
        xb = [R2[:, 256 * i:256 * (i + 1)] for i in range(2)]
        xbT = [dims(R2[:, 512 + 256 * i:512 + 256 * (i + 1)], 2, P) for i in range(2)]
        braw = R1[:, 0:96]
        brest = R1[:, 96:192]
        bparts = [R1[:, 192 + 48 * i:192 + 48 * (i + 1)].bitcast(BF16) for i in range(3)]
        selraw = dims(R1[0:9, 512:512 + 3 * P], 3, P)
        stats = dims(small[:, 0:30], NT, 6)
        mv = dims(small[:, 30:40], NT, 2)
        ve = small[:, 40:45]
        rstd = small[:, 45:50]
        mhalf = small[:, 50:55]
        nmax = small[:, 55:71]
        rinv = small[:, 71:87]
        sbu = small[:, 88:96]
        gb = small[:, 96:100]

        PS = ctx.enter_context(nc.psum_tensor("psum", [P, 8, 512], F32))
        ps_flat = PS[:, :, :].rearrange("p b n -> p (b n)")
        LN_BANK = (5, 7)
        V_BANK = (4, 5, 7)
        ctx_ps = dims(PS[:, 6, 0:HEADS * VW], HEADS, VW)

        in_patch, in_tokw, in_const, in_small = sem("in_patch"), sem("in_tokw"), sem("in_const"), sem("in_small")
        in_attn, in_abias, in_gate = sem2("in_attn"), sem2("in_abias"), sem2("in_gate")
        in_bias = sem("in_bias")
        in_shared, in_experts, in_last = sem("in_shared"), sem2("in_experts"), sem2("in_last")
        s_clear, s_psum0, s_zero = sem("s_clear"), sem("s_psum0"), sem("s_zero")
        s_braw, s_bsplit, s_bdram, s_bplace, s_sel = (sem(n) for n in ("s_braw", "s_bsplit", "s_bdram", "s_bplace", "s_sel"))
        s_dve = sem("dve_chain")
        s_embed, s_h0 = sem("s_embed"), sem("s_h0")
        s_ve = [sem(f"s_ve_{k}") for k in range(5)]
        s_rstd = [sem(f"s_rstd_{k}") for k in range(5)]
        s_xln = [sem(f"s_xln_{k}") for k in range(5)]
        s_tr = [sem(f"s_tr_{k}") for k in range(5)]
        s_xnT = [sem(f"s_xnT_{k}") for k in range(5)]
        s_qk, s_qkev, s_v, s_vev, s_vones, s_x3 = sem2("s_qk"), sem2("s_qkev"), sem2("s_v"), sem2("s_vev"), sem2("s_vones"), sem2("s_x3")
        s_kb = sem2("s_kb")
        s_scores, s_sadd, s_sub, s_exp = sem2("s_scores"), sem2("s_sadd"), sem2("s_sub"), sem2("s_exp")
        s_pt, s_ptev, s_pv, s_norm = sem2("s_pt"), sem2("s_ptev"), sem2("s_pv"), sem2("s_norm")
        s_ct, s_ctev, s_proj, s_res, s_hb = sem2("s_ct"), sem2("s_ctev"), sem2("s_proj"), sem2("s_res"), sem2("s_hb")
        s_logit, s_z, s_sig, s_mask, s_rank, s_pos, s_slots = (
            sem2(n) for n in ("s_logit", "s_z", "s_sig", "s_mask", "s_rank", "s_pos", "s_slots"))
        s_shup, s_shact, s_shdown, s_shev, s_hb2 = (sem(n) for n in ("s_shup", "s_shact", "s_shdown", "s_shev", "s_hb2"))
        s_scat = sem2("s_scat")
        s_xb = [sem2(f"s_xb{L}") for L in range(2)]
        s_ys = [sem2(f"s_ys{L}") for L in range(2)]
        s_xtr, s_xtev, s_up, s_silu, s_act = sem2("s_xtr"), sem2("s_xtev"), sem2("s_up"), sem2("s_silu"), sem2("s_act")
        s_atr, s_atev, s_down, s_yev = sem2("s_atr"), sem2("s_atev"), sem2("s_down"), sem2("s_yev")
        s_back = [[sem(f"s_back_{L}_{t}") for t in range(NT)] for L in range(2)]
        s_comb = sem2("s_comb")
        s_pad = sem("s_pad")
        s_out = sem("s_out")

        def block_steps(L, eng, first, step):
            first()
            step(0, 0, 0)
            step(1, 1, 1)
            turns = (ALWAYS - 2) // 2
            with eng.Fori(1, turns + 1) as i:
                step(i * 2, 0, 2)
                step(i * 2 + 1, 1, 3)
            for b in range(2 * turns + 2, ALWAYS):
                step(b, b % 2, b)
            eng.wait_ge(s_slots[L], 1)
            used = eng.value_load(be_i[0:1, BLOCKS_USED:BLOCKS_USED + 1], min_val=ALWAYS, max_val=BLOCKS[L])
            used_reg = eng.to_reg(used)
            for b in range(ALWAYS, BLOCKS[L]):
                with eng.If_cmp(used_reg, b, 'IS_GT'):
                    step(b, b % 2, b)

        block = ctx.enter_context(nc.Block())

        @block.sync
        def _(sp):
            for c in range(3):
                sp.dma_start(patch[:, 2 * c:2 * c + 2, :], a["patches"][:, 2 * c:2 * c + 2, :]).then_inc(in_patch, 16)
                sp.dma_start(tokw[:, 2 * c:2 * c + 2, :], a["tok_w"][:, 2 * c:2 * c + 2, :]).then_inc(in_tokw, 16)
            sp.dma_start(cst[:, :], a["consts"]).then_inc(in_const, 16)
            sp.dma_start(wA[:, 0:256], a["wq0"]).then_inc(in_attn[0], 16)
            sp.dma_start(wA[:, 512:768], a["wk0"]).then_inc(in_attn[0], 16)
            sp.dma_start(wA[:, 1024:1152], a["wv0"]).then_inc(in_attn[0], 16)
            sp.dma_start(wA[:, 1536:2048], a["wo0"]).then_inc(in_attn[0], 16)
            sp.dma_start(bp, a["bp"].partition_broadcast(P)).then_inc(in_small, 16)
            sp.dma_start(sbd, a["sbd"].partition_broadcast(P)).then_inc(in_small, 16)
            sp.dma_start(sbu, a["sbu"]).then_inc(in_small, 16)
            sp.dma_start(gb, a["gamma_beta"]).then_inc(in_small, 16)
            sp.dma_start(braw, a["biases"]).then_inc(s_braw, 16)
            sp.dma_start(selraw, a["select"]).then_inc(s_braw, 16)
            sp.dma_start(gateT[:, :, 0:8], a["gate0"]).then_inc(in_gate[0], 16)
            sp.dma_start(gbias[:, 0:8], a["gbias0"].partition_broadcast(P)).then_inc(in_gate[0], 16)
            sp.dma_start(abias[:, :], a["attn_bias0"]).then_inc(in_abias[0], 16)
            sp.wait_ge(s_clear, 1)
            for L in range(2):
                sp.dma_start(a["xs"][L].rearrange("(b p) d -> p b d", p=P),
                             zeros.unsqueeze(1).broadcast_to([P, BLOCKS[L], D])).then_inc(s_zero, 16)
                n = BLOCKS[L] - ALWAYS
                sp.dma_start(a["ys"][L].rearrange("(b p) d -> p b d", p=P)[:, ALWAYS:, :],
                             zeros.unsqueeze(1).broadcast_to([P, n, D])).then_inc(s_zero, 16)
            sp.wait_ge(s_bsplit, 3)
            for i in range(3):
                sp.dma_start(a["bias_parts"][i].rearrange("(p n) -> p n", p=P), bparts[i]).then_inc(s_bdram, 16)
            sp.dma_start(slot(0, 0, 4096), a["experts0"][0]).then_inc(in_shared, 16)
            for s in range(1, 7):
                sp.dma_start(slot(s, 0, 4096), a["experts0"][s]).then_inc(in_experts[0], 16)
            sp.wait_ge(s_bdram, 48)

            def place_biases(e0, e1):
                wb = W[:, :].bitcast(BF16)
                spare = dims(wb[0:9, :], 9, 2 * SLOT)
                for seg in range(3):
                    src = a["bias_parts"].rearrange("j (e s n) -> s j e n", e=8, s=3)[seg, :, e0:e1, :]
                    sp.dma_start(spare[3 * seg:3 * seg + 3, 1 + e0:1 + e1, 8192:8704], src).then_inc(in_bias, 16)

            place_biases(0, 6)
            sp.wait_ge(s_proj[0], NT)
            for s in range(7, 9):
                sp.dma_start(slot(s, 0, 4096), a["experts0"][s]).then_inc(in_last[0], 16)
            place_biases(6, 8)
            sp.dma_start(wA[:, 0:512], a["wq1"]).then_inc(in_attn[1], 16)
            sp.dma_start(wA[:, 512:1024], a["wk1"]).then_inc(in_attn[1], 16)
            sp.dma_start(wA[:, 1024:1536], a["wv1"]).then_inc(in_attn[1], 16)
            sp.dma_start(wA[:, 1536:2048], a["wo1"]).then_inc(in_attn[1], 16)
            sp.dma_start(abias[:, :], a["attn_bias1"]).then_inc(in_abias[1], 16)

            def rows(L):
                def load(b, par, k):
                    if k >= 2:
                        sp.wait_ge(s_xtr[L], b - 1)
                    sp.dma_start(xb[par], a["xs"][L][bass.ds(b * P, P), :]).then_inc(s_xb[L][par], 16)

                def step(b, par, k):
                    if k < BLOCKS[L] - 2:
                        load(b + 2, par, 2)
                    sp.wait_ge(s_yev[L], b + 1)
                    sp.dma_start(a["ys"][L][bass.ds(b * P, P), :], ys[par]).then_inc(s_ys[L][par], 16)

                def first():
                    sp.wait_ge(s_scat[L], 16 * 2 * NT)
                    load(0, 0, 0)
                    load(1, 1, 1)

                block_steps(L, sp, first, step)

            rows(0)
            sp.dma_start(gateT[:, :, :], a["gate1"]).then_inc(in_gate[1], 16)
            sp.dma_start(gbias[:, :], a["gbias1"].partition_broadcast(P)).then_inc(in_gate[1], 16)
            sp.wait_ge(s_proj[1], NT)
            for s in range(7, 9):
                sp.dma_start(slot(s, 0, SLOT), a["experts1"][s]).then_inc(in_last[1], 16)
            rows(1)
            for t in range(NT):
                sp.wait_ge(s_comb[1], 2 * (t + 1))
                sp.dma_start(out[t * P:t * P + ROWS[t], :], h[0:ROWS[t], t, :]).then_inc(s_out, 16)
            sp.wait_ge(s_out, 16 * NT)

        @block.gpsimd
        def _(g):
            def power(k):
                g.wait_ge(s_ve[k], 1)
                nc.gpsimd.tensor_tensor(rstd, ve, mhalf, ALU.pow).then_inc(s_rstd[k], 1)

            def key_blocks(L):
                g.wait_ge(s_qkev[L], 4 * CH[L])
                km = dims(const(f"kmask{L}"), 2, HB)
                for p in range(PAIRS):
                    if p >= 2:
                        g.wait_ge(s_scores[L], p - 1)
                    for u in range(2):
                        keys = dims(kT[:, u if L else 0, 72 * p:72 * (p + 1)], 2, PATCHES)
                        nc.gpsimd.tensor_tensor(
                            kb[p % 2][:, u, :, :].rearrange("p i (h k) -> p i h k", h=HB),
                            keys.unsqueeze(2).broadcast_to([P, 2, HB, PATCHES]),
                            km[:, u, :].unsqueeze(1).unsqueeze(3).broadcast_to([P, 2, HB, PATCHES]),
                            ALU.mult).then_inc(s_kb[L], 1)

            def scatter(L, k_ln):
                g.wait_ge(s_zero, 64)
                g.wait_ge(s_pos[L], 2)
                for k in range(2):
                    for t in range(NT):
                        n = ROWS[t]
                        g.indirect_dma_start(
                            a["xs"][L], bass.IndirectOffsetOnAxis(pos_i[0:n, k, t:t + 1].bitcast(U32), 0),
                            xln[0:n, t, :], None).then_inc(s_scat[L], 16)

            def gather(L):
                used = g.value_load(be_i[0:1, BLOCKS_USED:BLOCKS_USED + 1], min_val=ALWAYS, max_val=BLOCKS[L])

                def through(b):
                    g.wait_ge(s_ys[L][b % 2], 16 * (b // 2 + 1))
                    g.wait_ge(s_act[L], 2 * min(b + 2, BLOCKS[L]))

                through(ALWAYS - 2)
                through(ALWAYS - 1)
                used_reg = g.to_reg(used)
                for b in range(ALWAYS, BLOCKS[L]):
                    with g.If_cmp(used_reg, b, 'IS_GT'):
                        through(b)
                for t in range(NT):
                    for k in range(2):
                        m = ROWS[t]
                        g.indirect_dma_start(
                            back[0:m, k, t, :], None, a["ys"][L],
                            bass.IndirectOffsetOnAxis(pos_i[0:m, k, t:t + 1].bitcast(U32), 0),
                        ).then_inc(s_back[L][t], 16)

            g.wait_ge(s_clear, 3)
            power(0)
            g.wait_ge(s_xln[0], NT)
            g.wait_ge(in_small, 64)
            nc.gpsimd.tensor_tensor(h, h, bp.unsqueeze(1).broadcast_to([P, NT, D]), ALU.add).then_inc(s_hb[0], 1)
            g.wait_ge(in_const, 16)
            key_blocks(0)
            power(1)
            nc.gpsimd.tensor_scalar(sbd, sbd, 0.1, None, ALU.mult).then_inc(s_hb2, 1)
            g.wait_ge(s_hb2, 1)
            g.wait_ge(s_xln[1], NT)
            nc.gpsimd.tensor_tensor(h, h, sbd.unsqueeze(1).broadcast_to([P, NT, D]), ALU.add).then_inc(s_hb2, 1)
            scatter(0, 1)
            def load_expert(s):
                g.dma_start(slot(s, 0, SLOT), a["experts1"][s]).then_inc(in_experts[1], 16)

            g.wait_ge(s_shdown, NT)
            load_expert(0)
            g.wait_ge(s_down[0], NT)
            load_expert(1)
            g.wait_ge(s_slots[0], 1)
            gather(0)
            for s in range(2, 7):
                load_expert(s)
            power(2)
            power(3)
            g.wait_ge(s_xln[2], NT)
            nc.gpsimd.tensor_tensor(h, h, xln, ALU.add).then_inc(s_hb[1], 1)
            key_blocks(1)
            power(4)
            scatter(1, 4)
            g.wait_ge(s_slots[1], 1)
            gather(1)

        @block.tensor
        def _(pe):
            mm = nc.tensor.matmul

            def transposes_ln(k, src):
                for t in range(NT):
                    n = ROWS[t]
                    pe.wait_ge(s_xln[k], t + 1)
                    if t >= 2:
                        pe.wait_ge(s_xnT[k], t - 1)
                    for c in range(2):
                        last = nc.tensor.transpose(PS[:, LN_BANK[t % 2], c * P:c * P + n],
                                                   src[0:n, t, c * P:(c + 1) * P], ident[0:n, 0:n])
                    last.then_inc(s_tr[k], 1)

            def attention(L, k_ln):
                dq = DQ[L]
                pe.wait_ge(in_attn[L], 64)
                pe.wait_ge(s_xnT[k_ln], NT)
                items = [(w[L], c, i) for w in (wq, wk) for c in range(CH[L]) for i in range(2)]
                for i, (w, c, half) in enumerate(items):
                    if i >= 4:
                        pe.wait_ge(s_qkev[L], i - 3)
                    for k in range(2):
                        last = mm(PS[:, i % 4, 0:HALF], w[:, k, c * P:(c + 1) * P],
                                  xnT[:, k, half * HALF:(half + 1) * HALF], start=(k == 0), stop=(k == 1))
                    last.then_inc(s_qk[L], 1)
                pe.wait_ge(s_x3[L], 2)
                for i in range(IMGS):
                    if i >= 3:
                        pe.wait_ge(s_vev[L], i - 2)
                    for k in range(2):
                        last = mm(PS[0:108, V_BANK[i % 3], 0:VCOLS[L]],
                                  x3[k][:, i, :, :].rearrange("p r q -> p (r q)"), wv[L][:, k, :],
                                  start=(k == 0), stop=(k == 1))
                    last.then_inc(s_v[L], 1)

                def scores(p):
                    pe.wait_ge(s_kb[L], 2 * (p + 1))
                    if p >= 2:
                        pe.wait_ge(s_sadd[L], p - 1)
                    for u in range(2):
                        for par in range(2):
                            at = (2 * p + par) * PATCHES
                            last = mm(PS[64 * par:64 * par + PATCHES, 2 * (p % 2) + u, 0:HB * PATCHES],
                                      qT[:, u if L else 0, at:at + PATCHES], kb[p % 2][:, u, par, :],
                                      start=True, stop=True)
                    last.then_inc(s_scores[L], 1)

                def prob_turn(p):
                    pe.wait_ge(s_exp[L], p + 1)
                    if p >= 1:
                        pe.wait_ge(s_ptev[L], 2 * p)
                    else:
                        pe.wait_ge(s_vev[L], IMGS)
                    for g, (h0, nh) in enumerate(GROUPS):
                        last = nc.tensor.transpose(
                            ps_flat[0:nh * PATCHES, 4 * 512 + g * P:4 * 512 + (g + 1) * P],
                            prob[p % 2][:, h0 * PATCHES:(h0 + nh) * PATCHES], ident)
                    last.then_inc(s_pt[L], 1)

                def values(p):
                    pe.wait_ge(s_ptev[L], 2 * (p + 1))
                    if p >= 1:
                        pe.wait_ge(s_norm[L], p)
                    else:
                        pe.wait_ge(s_vones[L], 2)
                    for par in range(2):
                        for g, (h0, nh) in enumerate(GROUPS):
                            k = nh * PATCHES
                            last = mm(PS[64 * par:64 * par + PATCHES, 6, h0 * VW:(h0 + nh) * VW],
                                      pT[p % 2][0:k, g, par * PATCHES:(par + 1) * PATCHES],
                                      vblk[0:k, 2 * p + par, h0:h0 + nh, :], start=True, stop=True)
                    last.then_inc(s_pv[L], 1)

                def ctx_turn(p):
                    pe.wait_ge(s_norm[L], p + 1)
                    if p >= 1:
                        pe.wait_ge(s_ctev[L], p)
                    for c in range(2):
                        last = nc.tensor.transpose(PS[:, 7, c * P:(c + 1) * P],
                                                   ctxn[p % 2][:, c * P:(c + 1) * P], ident)
                    last.then_inc(s_ct[L], 1)

                scores(0)
                scores(1)
                for i in range(PAIRS + 1):
                    if i < PAIRS:
                        prob_turn(i)
                    if i < PAIRS - 2:
                        scores(i + 2)
                    if i >= 1:
                        ctx_turn(i - 1)
                    if i < PAIRS:
                        values(i)
                pe.wait_ge(s_ctev[L], PAIRS)
                for t in range(NT):
                    n = ROWS[t]
                    for k in range(2):
                        last = mm(PS[0:n, t, 0:D], ctxT[:, k, t * P:t * P + n], wo[:, k, :],
                                  start=(k == 0), stop=(k == 1))
                    last.then_inc(s_proj[L], 1)

            def logits(L, k_ln):
                pe.wait_ge(in_gate[L], 32)
                pe.wait_ge(s_xnT[k_ln], NT)
                for t in range(NT):
                    n = ROWS[t]
                    for k in range(2):
                        last = mm(PS[0:n, 7, 16 * t:16 * t + EXPERTS[L]], xnT[:, k, t * P:t * P + n],
                                  gateT[:, k, 0:EXPERTS[L]], start=(k == 0), stop=(k == 1))
                last.then_inc(s_logit[L], 1)

            def ranks(L):
                E = EXPERTS[L]
                pe.wait_ge(s_mask[L], 1)
                mm(PS[:, 6, 0:(NT + 1) * E], tri_b[:, :], mask_b[:, :, 0:E], start=True, stop=False)
                for u in range(NT):
                    last = mm(PS[:, 6, (u + 1) * E:(NT + 1) * E], ones_b[:, :],
                              mask_b[:, u:u + 1, 0:E].broadcast_to([P, NT - u, E]), start=False, stop=(u == NT - 1))
                last.then_inc(s_rank[L], 1)

            def shared_up():
                pe.wait_ge(in_shared, 16)
                for i in range(16):
                    c, half = i // 2, i % 2
                    if i >= 4:
                        pe.wait_ge(s_shact, i - 3)
                    for k in range(2):
                        last = mm(PS[:, i % 4, 0:HALF], slot(0, k * 1024 + c * P, P),
                                  xnT[:, k, half * HALF:(half + 1) * HALF], start=(k == 0), stop=(k == 1))
                    last.then_inc(s_shup, 1)

            def shared_down():
                pe.wait_ge(s_shact, 16)
                for t in range(NT):
                    n = ROWS[t]
                    if t >= 2:
                        pe.wait_ge(s_shev, t - 1)
                    for f in range(8):
                        last = mm(PS[0:n, 4 + t % 2, 0:D], shT[:, f, t * P:t * P + n],
                                  slot(0, 2048 + f * D, D), start=(f == 0), stop=(f == 7))
                    last.then_inc(s_shdown, 1)

            def experts(L):
                seg = SEG[L]
                wb = W[:, :].bitcast(BF16)

                def rows_turn(b, par, k):
                    pe.wait_ge(s_xb[L][par], (b // 2 + 1) * 16 if isinstance(b, int) else (b - par) * 8 + 16)
                    if k >= 1:
                        pe.wait_ge(s_xtev[L], b)
                    for c in range(2):
                        last = nc.tensor.transpose(PS[:, 7, c * P:(c + 1) * P],
                                                   xb[par][:, c * P:(c + 1) * P], ident)
                    last.then_inc(s_xtr[L], 1)

                def expert_of(b):
                    return pe.value_load(be_i[0:1, bass.ds(b, 1)], min_val=0, max_val=8)

                def up(b, par, k, s, e):
                    pe.wait_ge(s_xtev[L], b + 1)
                    if k >= 1:
                        pe.wait_ge(s_act[L], 2 * b + s - 1)
                    for part in range(L + 1):
                        bank = s + 2 * part
                        for c in range(2):
                            off = e * SLOT + part * 2 * HID[L] + c * HID[L] + s * seg
                            last = mm(PS[:, bank, 0:seg], xbT[par][:, c, :], W[:, bass.ds(off, seg)],
                                      start=(c == 0), stop=(L == 1 and c == 1))
                        if L == 0:
                            last = mm(PS[:, bank, 0:seg], sel[:, s, :], wb[0:9, bass.ds(e * 2 * SLOT + 8192, seg)],
                                      start=False, stop=True)
                    last.then_inc(s_up[L], 1)

                def act_turn(b, par, k):
                    pe.wait_ge(s_act[L], 2 * b + 2)
                    if k >= 1:
                        pe.wait_ge(s_atev[L], 2 * b)
                    elif L == 0:
                        pe.wait_ge(s_shev, NT)
                    for f in range(FCH[L]):
                        last = nc.tensor.transpose(ps_flat[:, 4 * 512 + f * P:4 * 512 + (f + 1) * P],
                                                   act[par][:, f * P:(f + 1) * P], ident)
                        if f in (3, FCH[L] - 1):
                            last.then_inc(s_atr[L], 1)

                def down(b, par, k, e):
                    pe.wait_ge(s_atev[L], 2 * b + 2)
                    if k >= 1:
                        pe.wait_ge(s_yev[L], b)
                    base = 2 * HID[L] * (L + 1)
                    y = PS[:, 6, 0:D]
                    for f in range(FCH[L]):
                        last = mm(y, actT[:, f * P:(f + 1) * P], W[:, bass.ds(e * SLOT + base + f * D, D)],
                                  start=(f == 0), stop=(L == 1 and f == FCH[L] - 1))
                    if L == 0:
                        last = mm(y, sel[:, 2, :], wb[0:9, bass.ds(e * 2 * SLOT + 8192, D)], start=False, stop=True)
                    last.then_inc(s_down[L], 1)

                def step(b, par, k):
                    more = k < BLOCKS[L] - 1
                    if more:
                        e1 = expert_of(b + 1)
                        up(b + 1, 1 - par, 1, 0, e1)
                    act_turn(b, par, k)
                    if more:
                        up(b + 1, 1 - par, 1, 1, e1)
                    if k < BLOCKS[L] - 2:
                        rows_turn(b + 2, par, 2)
                    down(b, par, k, expert_of(b))
                    if k >= ALWAYS - 1:
                        pe.wait_ge(s_xtev[L], min(b + 3, BLOCKS[L]))

                def first():
                    pe.wait_ge(s_slots[L], 1)
                    rows_turn(0, 0, 0)
                    rows_turn(1, 1, 1)
                    pe.wait_ge(in_experts[L], 16 * (6 + L))
                    pe.wait_ge(in_last[L], 32)
                    if L == 0:
                        pe.wait_ge(in_bias, 16 * 6)
                        pe.wait_ge(s_sel, 1)
                    e0 = expert_of(0)
                    up(0, 0, 0, 0, e0)
                    up(0, 0, 0, 1, e0)

                block_steps(L, pe, first, step)

            pe.wait_ge(s_psum0, 1)
            pe.wait_ge(in_patch, 48)
            pe.wait_ge(in_tokw, 48)
            for t in range(NT):
                n = ROWS[t]
                for k in range(6):
                    last = mm(PS[0:n, t, 0:D], patch[:, k, t * P:t * P + n], tokw[:, k, :],
                              start=(k == 0), stop=(k == 5))
                last.then_inc(s_embed, 1)
            pe.wait_ge(in_const, 16)
            transposes_ln(0, xln)
            attention(0, 0)
            transposes_ln(1, xln)
            logits(0, 1)
            shared_up()
            ranks(0)
            shared_down()
            experts(0)
            transposes_ln(3, xln2)
            attention(1, 3)
            transposes_ln(4, xln)
            logits(1, 4)
            ranks(1)
            experts(1)

        @block.scalar
        def _(ac):
            def copies_ln(k, affine=False):
                for t in range(NT):
                    n = ROWS[t]
                    ac.wait_ge(s_tr[k], t + 1)
                    src = dims(PS[:, LN_BANK[t % 2], 0:256], 2, P)[:, :, 0:n]
                    if not affine:
                        nc.scalar.copy(xnT[:, :, t * P:t * P + n], src).then_inc(s_xnT[k], 1)
                        continue
                    nc.scalar.activation(xnT[:, 0, t * P:t * P + n], src[:, 0, :], ACT.Identity,
                                         bias=gb[:, 2:3], scale=gb[:, 0:1])
                    nc.scalar.activation(xnT[:, 1, t * P:t * P + n], src[:, 1, :], ACT.Identity,
                                         bias=gb[:, 3:4], scale=gb[:, 1:2]).then_inc(s_xnT[k], 1)

            def attention(L, k_ln):
                ac.wait_ge(s_xnT[k_ln], NT)
                nc.scalar.copy(x3[1], dims(xnT[:, 1, :], IMGS, PATCHES).unsqueeze(2).broadcast_to(
                    [P, IMGS, 3, PATCHES])).then_inc(s_x3[L], 1)
                for i in range(4 * CH[L]):
                    ac.wait_ge(s_qk[L], i + 1)
                    c, half = i // 2 % CH[L], i % 2
                    part = slice(half * HALF, (half + 1) * HALF)
                    if i < 2 * CH[L]:
                        nc.scalar.mul(qT[:, c, part], PS[:, i % 4, 0:HALF], QSCALE[L]).then_inc(s_qkev[L], 1)
                    else:
                        if L == 0 and i == 2 * CH[L]:
                            ac.wait_ge(s_bdram, 48)
                            ac.wait_ge(s_sel, 1)
                        nc.scalar.copy(kT[:, c, part], PS[:, i % 4, 0:HALF]).then_inc(s_qkev[L], 1)

                def exp(p):
                    ac.wait_ge(s_sub[L], p + 1)
                    nc.scalar.activation(prob[p % 2], prob[p % 2], ACT.Exp).then_inc(s_exp[L], 1)

                def prob_out(p):
                    ac.wait_ge(s_pt[L], p + 1)
                    if p >= 2:
                        ac.wait_ge(s_pv[L], p - 1)
                    src = dims(ps_flat[:, 4 * 512:4 * 512 + 6 * P], 6, 2, 64)
                    for g0, g1, k in ((0, 5, 108), (5, 6, PATCHES)):
                        dst = pT[p % 2][0:k, g0:g1, :].rearrange("p g (i q) -> p g i q", i=2)
                        nc.scalar.copy(dst, src[0:k, g0:g1, :, 0:PATCHES]).then_inc(s_ptev[L], 1)

                def ctx_out(p):
                    ac.wait_ge(s_ct[L], p + 1)
                    src = dims(PS[:, 7, 0:256], 2, 2, 64)[:, :, :, 0:PATCHES]
                    dst = ctxT[:, :, 72 * p:72 * (p + 1)].rearrange("p c (i q) -> p c i q", i=2)
                    nc.scalar.copy(dst, src).then_inc(s_ctev[L], 1)

                exp(0)
                for i in range(PAIRS + 1):
                    if i < PAIRS - 1:
                        exp(i + 1)
                    if i < PAIRS:
                        prob_out(i)
                    if i >= 1:
                        ctx_out(i - 1)

            def sigmoid(L):
                E = EXPERTS[L]
                ac.wait_ge(s_z[L], 1)
                nc.scalar.activation(rt[:, 2 * 45:2 * 45 + NT * E], rt[:, 45:45 + NT * E],
                                     ACT.Sigmoid).then_inc(s_sig[L], 1)

            def experts(L):
                seg = SEG[L]

                def rows_copy(b, par, k):
                    ac.wait_ge(s_xtr[L], b + 1)
                    if k >= 2:
                        ac.wait_ge(s_up[L], 2 * b - 2)
                    nc.scalar.copy(xbT[par], dims(PS[:, 7, 0:256], 2, P)
                                   ).then_inc(s_xtev[L], 1)

                def gate(b, par, k, s):
                    ac.wait_ge(s_up[L], 2 * b + s + 1)
                    if k >= 2:
                        ac.wait_ge(s_atr[L], 2 * b - 2)
                    nc.scalar.activation(act[par][:, s * seg:(s + 1) * seg], PS[:, s, 0:seg],
                                         ACT.Silu if L else ACT.Gelu).then_inc((s_silu if L else s_act)[L], 1)

                def step(b, par, k):
                    if k < BLOCKS[L] - 1:
                        gate(b + 1, 1 - par, k + 1, 0)
                        gate(b + 1, 1 - par, k + 1, 1)
                    if k < BLOCKS[L] - 2:
                        rows_copy(b + 2, par, 2)

                def first():
                    rows_copy(0, 0, 0)
                    rows_copy(1, 1, 1)
                    if L == 1:
                        ac.wait_ge(s_pad, 1)
                    gate(0, 0, 0, 0)
                    gate(0, 0, 0, 1)

                block_steps(L, ac, first, step)

            copies_ln(0)
            attention(0, 0)
            copies_ln(1)
            sigmoid(0)
            ac.wait_ge(in_small, 64)
            for i in range(16):
                c, half = i // 2, i % 2
                ac.wait_ge(s_shup, i + 1)
                nc.scalar.activation(shT[:, c, half * HALF:(half + 1) * HALF], PS[:, i % 4, 0:HALF],
                                     ACT.Gelu, bias=sbu[:, c:c + 1]).then_inc(s_shact, 1)
            experts(0)
            copies_ln(3, affine=True)
            attention(1, 3)
            copies_ln(4)
            sigmoid(1)
            experts(1)

        @block.vector
        def _(v):
            chained = [0]

            def link(ins):
                chained[0] += 1
                ins.then_inc(s_dve, 1)
                v.wait_ge(s_dve, chained[0])

            TT, TS, STT = nc.vector.tensor_tensor, nc.vector.tensor_scalar, nc.vector.scalar_tensor_tensor

            def layernorm(k, src, dst):
                for t in range(NT):
                    last = nc.vector.bn_stats(stats[:, t, :], src[:, t, :])
                link(last)
                for t in range(NT):
                    last = nc.vector.bn_aggr(mv[:, t, :], stats[:, t, :])
                link(last)
                TS(ve, mv[:, :, 1], EPS_LN, None, ALU.add).then_inc(s_ve[k], 1)
                v.wait_ge(s_rstd[k], 1)
                for t in range(NT):
                    TS(dst[:, t, :], src[:, t, :], mv[:, t, 0:1], rstd[:, t:t + 1], ALU.subtract,
                       ALU.mult).then_inc(s_xln[k], 1)

            def attention(L, k_ln):
                mask = const("vmask")[0:108, :]
                v.wait_ge(s_xnT[k_ln], NT)
                nc.vector.tensor_copy(x3[0], dims(xnT[:, 0, :], IMGS, PATCHES).unsqueeze(2).broadcast_to(
                    [P, IMGS, 3, PATCHES])).then_inc(s_x3[L], 1)
                nc.vector.tensor_copy(vblk[0:108, :, :, DH],
                                      mask.unsqueeze(1).broadcast_to([108, IMGS, HEADS])).then_inc(s_vones[L], 1)
                nc.vector.memset(PS[:, 6, 0:HEADS * VW], 1.0).then_inc(s_vones[L], 1)
                for i in range(IMGS):
                    v.wait_ge(s_v[L], i + 1)
                    if L == 0:
                        dst = vblk[0:108, i, :, 0:DH].rearrange("p (j c) d -> p j c d", j=4)
                        src = dims(PS[0:108, V_BANK[i % 3], 0:64], 4, DH).unsqueeze(1).broadcast_to([108, 4, 4, DH])
                        m = dims(mask, 4, 4).unsqueeze(3).broadcast_to([108, 4, 4, DH])
                    else:
                        dst = vblk[0:108, i, :, 0:DH]
                        src = dims(PS[0:108, V_BANK[i % 3], 0:256], HEADS, DH)
                        m = mask.unsqueeze(2).broadcast_to([108, HEADS, DH])
                    TT(dst, src, m, ALU.mult).then_inc(s_vev[L], 1)
                v.wait_ge(in_abias[L], 16)

                def softmax(p):
                    t = prob[p % 2]
                    v.wait_ge(s_scores[L], p + 1)
                    if p >= 2:
                        v.wait_ge(s_pt[L], p - 1)
                    TT(dims(t, 2, HB * PATCHES), PS[:, 2 * (p % 2):2 * (p % 2) + 2, 0:HB * PATCHES],
                       dims(abias[:, :], 2, HB * PATCHES), ALU.add).then_inc(s_sadd[L], 1)
                    v.wait_ge(s_sadd[L], p + 1)
                    link(nc.vector.tensor_reduce(nmax, dims(t, HEADS, PATCHES), AX, ALU.max))
                    TT(dims(t, HEADS, PATCHES), dims(t, HEADS, PATCHES),
                       nmax.unsqueeze(2).broadcast_to([P, HEADS, PATCHES]), ALU.subtract).then_inc(s_sub[L], 1)

                def normalize(p):
                    v.wait_ge(s_pv[L], p + 1)
                    link(nc.vector.reciprocal(rinv, ctx_ps[:, :, DH]))
                    if p >= 2:
                        v.wait_ge(s_ct[L], p - 1)
                    elif L == 0:
                        v.wait_ge(s_zero, 64)
                    TT(dims(ctxn[p % 2], HEADS, DH), ctx_ps[:, :, 0:DH],
                       rinv.unsqueeze(2).broadcast_to([P, HEADS, DH]), ALU.mult).then_inc(s_norm[L], 1)

                softmax(0)
                softmax(1)
                for i in range(PAIRS):
                    if i < PAIRS - 2:
                        softmax(i + 2)
                    normalize(i)
                v.wait_ge(s_hb[L], 1)
                for t in range(NT):
                    n = ROWS[t]
                    v.wait_ge(s_proj[L], t + 1)
                    last = TT(h[0:n, t, :], PS[0:n, t, 0:D], h[0:n, t, :], ALU.add)
                link(last)

            def route(L):
                E = EXPERTS[L]

                def tmp(i):
                    return dims(rt[:, 45 * i:45 * i + NT * E], NT, E)

                M, z, sig, key, oh1, oh2, t1, t2 = (tmp(i) for i in range(8))
                r5 = [rt[:, 360 + 5 * i:365 + 5 * i] for i in range(8)]
                nb, cum, start = (rt[:, 400 + 9 * i:400 + 9 * i + E] for i in range(3))
                ids = const("ids")[:, 0:E].unsqueeze(1).broadcast_to([P, NT, E])

                def bc(x):
                    return x.unsqueeze(2).broadcast_to([P, NT, E])

                v.wait_ge(s_logit[L], 1)
                TT(z, dims(PS[:, 7, 0:80], NT, 16)[:, :, 0:E], gbias[:, 0:E].unsqueeze(1).broadcast_to([P, NT, E]),
                   ALU.add).then_inc(s_z[L], 1)
                v.wait_ge(s_z[L], 1)
                link(TS(key, z, 17.0, -103.0, ALU.min, ALU.max))
                for oh, m, i in ((oh1, r5[0], r5[1]), (oh2, r5[2], r5[3])):
                    link(nc.vector.tensor_reduce(m, key, AX, ALU.max))
                    link(TT(t1, key, bc(m), ALU.is_equal))
                    link(STT(t1, t1, -99.0, ids, ALU.mult, ALU.add))
                    link(nc.vector.tensor_reduce(i, t1, AX, ALU.min))
                    link(TS(i, i, 99.0, None, ALU.add))
                    link(TT(oh, ids, bc(i), ALU.is_equal))
                    if oh is oh1:
                        link(STT(key, oh1, -1e6, key, ALU.mult, ALU.add))
                link(TT(M, oh1, oh2, ALU.add))
                TT(mask_b[:, 0:NT, 0:E], M, bc(const("valid")), ALU.mult).then_inc(s_mask[L], 1)
                v.wait_ge(s_sig[L], 1)
                TT(t1, sig, oh1, ALU.mult)
                link(TT(t2, sig, oh2, ALU.mult))
                nc.vector.tensor_reduce(r5[0], t1, AX, ALU.add)
                link(nc.vector.tensor_reduce(r5[1], t2, AX, ALU.add))
                link(STT(r5[2], r5[0], EPS_TOPK[L], r5[1], ALU.add, ALU.add))
                link(nc.vector.reciprocal(r5[3], r5[2]))
                TT(pw[:, 0, :], r5[0], r5[3], ALU.mult)
                link(TT(pw[:, 1, :], r5[1], r5[3], ALU.mult))
                v.wait_ge(s_rank[L], 1)
                c5 = dims(rt[:, 45:45 + NT * E], E, NT)
                link(TT(c5, PS[:, 6, NT * E:(NT + 1) * E].unsqueeze(2).broadcast_to([P, E, NT]),
                        const("thr").unsqueeze(1).broadcast_to([P, E, NT]), ALU.is_gt))
                link(nc.vector.tensor_reduce(nb, c5, AX, ALU.add))
                ee = dims(rt[:, 90:90 + E * E], E, E)
                link(TT(ee, nb.unsqueeze(1).broadcast_to([P, E, E]), dims(const(f"le{L}"), E, E), ALU.mult))
                link(nc.vector.tensor_reduce(cum, ee, AX, ALU.add))
                link(TT(start, cum, nb, ALU.subtract))
                link(TS(start, start, float(P), None, ALU.mult))
                place = tmp(1)
                link(TT(place, dims(PS[:, 6, 0:NT * E], NT, E),
                        start.unsqueeze(1).broadcast_to([P, NT, E]), ALU.add))
                TT(t1, place, oh1, ALU.mult)
                link(TT(t2, place, oh2, ALU.mult))
                nc.vector.tensor_reduce(r5[4], t1, AX, ALU.add)
                link(nc.vector.tensor_reduce(r5[5], t2, AX, ALU.add))
                nc.vector.tensor_copy(pos_i[:, 0, :], r5[4]).then_inc(s_pos[L], 1)
                nc.vector.tensor_copy(pos_i[:, 1, :], r5[5]).then_inc(s_pos[L], 1)
                nb_, c1 = BLOCKS[L], rt[0:1, 90:90 + BLOCKS[L] * E]
                c1 = dims(c1, nb_, E)
                link(TT(c1, cum[0:1, :].unsqueeze(1).broadcast_to([1, nb_, E]),
                        const("blk")[0:1, 0:nb_].unsqueeze(2).broadcast_to([1, nb_, E]), ALU.is_le))
                bf = rt[0:1, 260:260 + nb_]
                link(nc.vector.tensor_reduce(bf, c1, AX, ALU.add))
                nc.vector.tensor_copy(be_i[:, BLOCKS_USED:BLOCKS_USED + 1], cum[0:1, E - 1:E])
                TS(be_i[:, 0:nb_], bf, float(E - 1), float(FIRST_SLOT[L]), ALU.min, ALU.add).then_inc(s_slots[L], 1)

            def experts(L):
                seg = SEG[L]

                def hidden(b, par, k, s):
                    v.wait_ge(s_silu[L], 2 * b + s + 1)
                    part = act[par][:, s * seg:(s + 1) * seg]
                    TT(part, part, PS[:, 2 + s, 0:seg], ALU.mult).then_inc(s_act[L], 1)

                def turned(b, par, k, half):
                    v.wait_ge(s_atr[L], 2 * b + half + 1)
                    if k >= 1:
                        v.wait_ge(s_down[L], b)
                    n = 512 if half == 0 else FCH[L] * P - 512
                    nc.vector.tensor_copy(actT[:, half * 512:half * 512 + n],
                                          PS[:, 4 + half, 0:n]).then_inc(s_atev[L], 1)

                def step(b, par, k):
                    if L == 1 and k < BLOCKS[L] - 1:
                        hidden(b + 1, 1 - par, k + 1, 0)
                    turned(b, par, k, 0)
                    turned(b, par, k, 1)
                    if L == 1 and k < BLOCKS[L] - 1:
                        hidden(b + 1, 1 - par, k + 1, 1)
                    v.wait_ge(s_down[L], b + 1)
                    if k >= 2:
                        v.wait_ge(s_ys[L][par], (b // 2) * 16 if isinstance(b, int) else (b - par) * 8)
                    nc.vector.tensor_copy(ys[par], PS[:, 6, 0:D]).then_inc(s_yev[L], 1)

                def first():
                    if L == 1:
                        hidden(0, 0, 0, 0)
                        hidden(0, 0, 0, 1)

                block_steps(L, v, first, step)

            def combine(L):
                for t in range(NT):
                    n = ROWS[t]
                    v.wait_ge(s_back[L][t], 32)
                    for k in range(2):
                        STT(h[0:n, t, :], back[0:n, k, t, :], pw[0:n, k, t:t + 1], h[0:n, t, :],
                            ALU.mult, ALU.add).then_inc(s_comb[L], 1)
                        v.wait_ge(s_comb[L], 2 * t + k + 1)

            nc.vector.memset(zeros, 0.0).then_inc(s_clear, 1)
            nc.vector.memset(h[64:P, NT - 1, :], 0.0).then_inc(s_clear, 1)
            nc.vector.memset(mhalf, -0.5).then_inc(s_clear, 1)
            nc.vector.memset(PS[:, :, :], 0.0).then_inc(s_psum0, 1)
            nc.vector.memset(ones_b[:, :], 1.0)
            nc.vector.memset(mask_b[:, :, :], 0.0)
            v.wait_ge(s_braw, 32)
            link(nc.vector.tensor_copy(bparts[0], braw))
            link(TT(brest, braw, bparts[0], ALU.subtract))
            link(nc.vector.tensor_copy(bparts[1], brest))
            link(TT(brest, brest, bparts[1], ALU.subtract))
            nc.vector.tensor_copy(bparts[2], brest).then_inc(s_bsplit, 3)
            nc.vector.tensor_copy(sel[:, :, :], selraw).then_inc(s_sel, 1)
            for t in range(NT):
                n = ROWS[t]
                v.wait_ge(s_embed, t + 1)
                last = nc.vector.tensor_copy(h[0:n, t, :], PS[0:n, t, 0:D])
            link(last)
            layernorm(0, h, xln)
            v.wait_ge(in_const, 16)
            nc.vector.tensor_copy(tri_b[:, :], const("tri"))
            attention(0, 0)
            layernorm(1, h, xln)
            route(0)
            v.wait_ge(s_hb2, 2)
            for t in range(NT):
                n = ROWS[t]
                v.wait_ge(s_shdown, t + 1)
                last = STT(h[0:n, t, :], PS[0:n, 4 + t % 2, 0:D], 0.1, h[0:n, t, :], ALU.mult, ALU.add)
                last.then_inc(s_shev, 1)
            v.wait_ge(s_shev, NT)
            experts(0)
            combine(0)
            layernorm(2, h, xln)
            v.wait_ge(s_xln[2], NT)
            layernorm(3, xln, xln2)
            attention(1, 3)
            layernorm(4, h, xln)
            for i in range(2):
                last = nc.vector.memset(act[i][:, HID[1]:FCH[1] * P], 0.0)
            last.then_inc(s_pad, 1)
            route(1)
            experts(1)
            combine(1)


def host_layout(x):
    import numpy as np

    def g(name):
        return np.asarray(x[name])

    def kp(w):
        return w.reshape(-1, P, w.shape[1]).transpose(1, 0, 2)

    def flat(w):
        return w.reshape(P, -1)

    o = {}
    img = g("x").reshape(IMGS, 3, 6, 16, 6, 16).transpose(0, 1, 3, 5, 2, 4)
    patches = img.reshape(IMGS, PATCHES, FEAT).transpose(2, 0, 1).reshape(FEAT, TOK)
    o["patches"] = kp(patches)
    o["tok_w"] = kp(g("L0_tok_W"))
    o["wq0"] = flat(kp(g("L0_attn_Wq")))
    o["wk0"] = flat(kp(np.tile(g("L0_attn_Wk"), (1, 4))))
    o["wv0"] = flat(kp(g("L0_attn_Wv")))
    o["wo0"] = flat(kp(g("L0_attn_Wp")))
    o["bp"], o["sbd"] = g("L0_attn_bp"), g("L0_ffn_sbd")
    o["sbu"] = g("L0_ffn_sbu").reshape(8, P).T
    o["wq1"] = flat(kp(g("L1_attn_Wq").T))
    o["wk1"] = flat(kp(g("L1_attn_Wk").T))
    o["wv1"] = flat(kp(g("L1_attn_Wv").T))
    o["wo1"] = flat(kp(g("L1_attn_Wo").T))
    o["gamma_beta"] = np.concatenate([g("L1_attn_ln_gamma").reshape(2, P).T, g("L1_attn_ln_beta").reshape(2, P).T], 1)
    o["gate0"] = kp(g("L0_ffn_gate_w").T)
    o["gbias0"] = g("L0_ffn_gate_bias")
    o["gate1"] = kp(np.concatenate([g("L1_ffn_gate_weight"), g("L1_ffn_new_gate_weight")]).T)
    o["gbias1"] = np.concatenate([np.zeros(8, np.float32), g("L1_ffn_gate_bias")])
    b = np.zeros((8, 1536), np.float32)
    b[:, :1024], b[:, 1024:1280] = g("L0_ffn_bu"), g("L0_ffn_bd")
    o["biases"] = b.reshape(P, 96)

    up0 = np.concatenate([g("L0_ffn_sWu")[None], g("L0_ffn_Wu")])
    dn0 = np.concatenate([g("L0_ffn_sWd")[None], g("L0_ffn_Wd")])
    o["experts0"] = np.stack([np.concatenate([flat(kp(up0[e].T)), flat(kp(dn0[e].T))], 1) for e in range(9)])
    w1 = np.concatenate([g("L1_ffn_w1"), g("L1_ffn_new_w1")])
    w2 = np.concatenate([g("L1_ffn_w2"), g("L1_ffn_new_w2")])
    w3 = np.concatenate([g("L1_ffn_w3"), g("L1_ffn_new_w3")])
    w2t = np.zeros((9, FCH[1] * P, D), np.float32)
    w2t[:, :HID[1]] = w2.transpose(0, 2, 1)
    o["experts1"] = np.stack([np.concatenate([flat(kp(w1[e].T)), flat(kp(w3[e].T)), flat(kp(w2t[e]))], 1)
                              for e in range(9)])

    i, j = np.arange(PATCHES)[:, None], np.arange(PATCHES)[None, :]
    causal = j > i
    slopes = (2.0 ** (-8.0 * np.arange(1, HEADS + 1) / HEADS)).astype(np.float32)
    alibi = (slopes[:, None, None] * (j - i).astype(np.float32) / np.float32(np.sqrt(8.0))).astype(np.float32)
    rel = g("L1_attn_rel")[:, np.clip(i - j, 0, 128)]
    for L, table in enumerate((alibi, rel)):
        slots = np.zeros((P, HEADS, PATCHES), np.float32)
        t = np.where(causal[None], np.float32(NEG), table).transpose(1, 0, 2)
        slots[0:PATCHES], slots[64:64 + PATCHES] = t, t
        o[f"attn_bias{L}"] = slots.reshape(P, -1)

    c = np.zeros((P, NCONST), np.float32)

    def put(name, value):
        at, n = CONST[name]
        c[:, at:at + n] = value

    put("ident", np.eye(P))
    put("tri", np.triu(np.ones((P, P)), 1))
    r = np.arange(P)
    put("vmask", (r[:, None] // PATCHES) == (np.arange(HEADS)[None] % 3))
    hs = np.arange(HEADS)[None]
    put("kmask0", (r[:, None] // DQ[0]) == hs)
    put("kmask1", (r[:, None] // DQ[1]) == hs % HB)
    put("le0", np.tril(np.ones((8, 8))).reshape(1, -1))
    put("le1", np.tril(np.ones((9, 9))).reshape(1, -1))
    put("thr", P * np.arange(NT)[None])
    put("valid", (r[:, None] + P * np.arange(NT)[None]) < TOK)
    put("ids", np.arange(9)[None])
    put("blk", np.arange(18)[None])
    o["consts"] = c
    s = np.zeros((9, 3, P), np.float32)
    for k in range(9):
        s[k, k // 3] = 1
    o["select"] = s
    return {k: np.ascontiguousarray(w) for k, w in o.items()}


def kernel(**inputs):
    import concourse.bacc as bacc
    from concourse.bass_utils import run_bass_kernel_spmd as run

    nc = bacc.Bacc("TRN2", target_bir_lowering=False, num_devices=1)
    arrays = {f"in_{k}": w for k, w in host_layout(inputs).items()}
    a = {k[3:]: nc.dram_tensor(k, w.shape, F32, kind="ExternalInput").ap() for k, w in arrays.items()}
    a["xs"] = [nc.dram_tensor(f"sorted_rows_{L}", (BLOCKS[L] * P, D), F32, kind="Internal").ap() for L in range(2)]
    a["ys"] = [nc.dram_tensor(f"expert_rows_{L}", (BLOCKS[L] * P, D), F32, kind="Internal").ap() for L in range(2)]
    a["bias_parts"] = nc.dram_tensor("bias_parts", (3, 8 * 1536), BF16, kind="Internal").ap()
    out = nc.dram_tensor("out", (TOK, D), F32, kind="ExternalOutput").ap()
    tower(nc, a, out)
    r = run(nc, [arrays], core_ids=[0])
    return r.results[0]["out"].reshape(IMGS, PATCHES, D)
```

```python
from contextlib import ExitStack

import concourse.bass as bass
from concourse import mybir

F32 = mybir.dt.float32
BF16 = mybir.dt.bfloat16
I32 = mybir.dt.int32
U32 = mybir.dt.uint32
ACT = mybir.ActivationFunctionType
ALU = mybir.AluOpType
AX = mybir.AxisListType.X

P = 128
IMGS, PATCHES, D, FEAT = 16, 36, 256, 768
TOK = IMGS * PATCHES
NT = -(-TOK // P)
ROWS = [min(P, TOK - t * P) for t in range(NT)]
HALF = TOK // 2
PAIRS = IMGS // 2
HEADS, DH = 16, 16
DQ = (8, 16)
CH = (1, 2)
LAG = 5
EARLY = (5, 9)
HB = 8
QSCALE = (8.0 ** -0.5, 16.0 ** -0.5)
GROUPS = [(3 * g, min(3, HEADS - 3 * g)) for g in range(-(-HEADS // 3))]
VW = DH + 1
EPS_LN = 1e-5
EXPERTS = (8, 9)
HID = (1024, 704)
FCH = (8, 6)
SEG = (512, 352)
BLOCKS = tuple((2 * TOK + e * (P - 1)) // P for e in EXPERTS)
ALWAYS = -(-2 * TOK // P)
BLOCKS_USED = 18
SLOT = 4352
EPS_TOPK = (1e-6, 1e-20)
TURNS = (((0, 6),), ((0, 3), (3, 6)))
DVE_COLS = 6
VALS = 6
FIRST_SLOT = (1, 0)
NEG = -1e30

CONST = {}
_at = 0
for _name, _n in (("ident", P), ("tri", P), ("vmask", HEADS), ("kmask0", HEADS), ("kmask1", HEADS),
                  ("before0", 64), ("before1", 81), ("thr", NT),
                  ("dump", 1), ("ids", 9), ("ids99", 9), ("blk", 18), ("edge", 18),
                  ("iota", P), ("vals", 2 * NT * VALS), ("minus_dump", 1)):
    CONST[_name] = (_at, _n)
    _at += _n
NCONST = _at


def dims(ap, *shape):
    names = "abcd"[:len(shape)]
    return ap.rearrange(f"p ({' '.join(names)}) -> p {' '.join(names)}", **dict(zip(names, shape)))


def tower(nc, a):
    ctx = ExitStack()
    with ctx:
        def sb(name, shape, dt=F32):
            return ctx.enter_context(nc.sbuf_tensor(name, shape, dt))

        def sem(name):
            return ctx.enter_context(nc.semaphore(name))

        def sem2(name):
            return [sem(f"{name}_{n}") for n in range(2)]

        W = sb("expert_slots", [P, 9 * SLOT])
        R1 = sb("phase_buffers", [P, 4864])
        R2 = sb("row_buffers", [P, 1024])
        wA = sb("attn_weights", [P, 2048])
        abias = sb("attn_bias", [P, HEADS * PATCHES])
        tri_b = sb("tri_bf16", [P, P], BF16)
        ones_b = sb("ones_bf16", [P, P], BF16)
        mask_b = sb("expert_mask", [P, NT + 1, 9], BF16)
        h_t = sb("h", [P, NT * D])
        x_t = sb("xln", [P, NT * D])
        xnT_t = sb("xnT", [P, 2 * TOK])
        cst = sb("consts", [P, NCONST])
        sel = sb("bias_select", [9, 3, P], BF16)
        small = sb("small", [P, 110])
        rt = sb("route", [P, 10 * 45])
        vals_b = sb("token_vals", [P, 2 * NT, VALS], BF16)
        gather_i = sb("gather_index", [P, max(BLOCKS)], I32)
        add_i = sb("add_index", [P, max(BLOCKS)], I32)
        be_i = sb("block_slots", [1, BLOCKS_USED + 1], I32)
        w_slot = sb("slot_weights", [P, max(BLOCKS)])
        gateT = sb("gateT", [P, 2, 9])
        gbias = sb("gate_bias", [P, 9])

        h = dims(h_t[:, :], NT, D)
        xln = dims(x_t[:, :], NT, D)
        xnT = dims(xnT_t[:, :], 2, TOK)

        def slot(s, off, n):
            return W[:, s * SLOT + off:s * SLOT + off + n]

        def const(name):
            o, n = CONST[name]
            return cst[:, o:o + n]

        ident = const("ident")
        vblk = dims(slot(7, 0, IMGS * HEADS * VW), IMGS, HEADS, VW)
        qT = dims(slot(8, 0, 2 * TOK), 2, TOK)
        kb = [dims(slot(8, 1152 + 1152 * i, 1152), 2, 2, HB * PATCHES) for i in range(2)]
        pT = [dims(slot(8, 3456 + 432 * i, 432), 6, 72) for i in range(2)]
        kT = dims(R1[:, 0:2 * TOK], 2, TOK)
        xln2 = dims(slot(7, 0, NT * D), NT, D)
        x3 = [dims(t, IMGS, 3, PATCHES) for t in (R1[:, 1152:1152 + 3 * TOK], R1[:, 2880:2880 + 3 * TOK])]
        v_t = dims(R1[:, 1152:1152 + NT * D], NT, D)
        vraw = [dims(R1[0:108, 2432 + 1024 * i:2432 + 1024 * (i + 1)], 4, HEADS, DH) for i in range(2)]
        ctxT = dims(R1[:, 2304:2304 + 2 * TOK], 2, TOK)
        prob = [x_t[:, 576 * i:576 * (i + 1)] for i in range(2)]
        ctxn = [R2[:, 256 * i:256 * (i + 1)] for i in range(2)]
        zeros = R2[:, 0:D]
        bp = R2[:, 768:1024]
        wq = [dims(wA[:, 0:256], 2, 128), dims(wA[:, 0:512], 2, 256)]
        wk = [dims(wA[:, 512:768], 2, 128), dims(wA[:, 512:1024], 2, 256)]
        wv = [dims(wA[:, 1024:1152], 2, 64), dims(wA[:, 1024:1536], 2, 256)]
        wo = dims(wA[:, 1536:2048], 2, 256)
        patch = dims(slot(7, 0, 6 * TOK), 6, TOK)
        tokw = dims(slot(8, 0, 6 * D), 6, D)
        shT = dims(R1[:, 0:8 * TOK], 8, TOK)
        sbd = R1[:, 4608:4864]
        act = [R1[:, 1024 * i:1024 * (i + 1)] for i in range(2)]
        actT = R1[:, 2048:3072]
        ys = [R1[:, 3072 + 256 * i:3072 + 256 * (i + 1)] for i in range(2)]
        xb = [R2[:, 256 * i:256 * (i + 1)] for i in range(2)]
        place_vals = abias[:, 0:NT * VALS * max(BLOCKS)].bitcast(BF16).rearrange(
            "p (j n) -> p j n", j=2 * NT)
        onehot = [t.bitcast(BF16).rearrange("p (j s) -> p j s", s=P) for t in (R2[:, 0:640], R1[:, 3584:4224])]
        xbT = [dims(R2[:, 512 + 256 * i:512 + 256 * (i + 1)], 2, P) for i in range(2)]
        braw = R1[:, 0:96]
        brest = R1[:, 96:192]
        bparts = [R1[:, 192 + 48 * i:192 + 48 * (i + 1)].bitcast(BF16) for i in range(3)]
        selraw = dims(R1[0:9, 512:512 + 3 * P], 3, P)
        stats = dims(small[:, 0:30], NT, 6)
        mv = dims(small[:, 30:40], NT, 2)
        ve = dims(small[:, 40:50], NT, 2)
        rstd = dims(small[:, 100:110], NT, 2)
        mhalf = small[:, 50:52]
        nmax = small[:, 55:71]
        rinv = small[:, 71:87]
        sbu = small[:, 88:96]
        gb = small[:, 96:100]

        PS = ctx.enter_context(nc.psum_tensor("psum", [P, 8, 512], F32))
        ps_flat = PS[:, :, :].rearrange("p b n -> p (b n)")
        LN_BANK = (5, 7)
        SH_BANK = (4, 5, 2, 3, 1)
        V_BANK = (4, 5, 7)
        ctx_ps = dims(PS[:, 6, 0:HEADS * VW], HEADS, VW)

        in_patch, in_const, in_small = [sem(f"in_patch_{c}") for c in range(6)], sem("in_const"), sem("in_small")
        in_attn, in_gate = sem2("in_attn"), sem("in_gate")
        in_bias = sem("in_bias")
        in_shared, in_experts, in_last = sem("in_shared"), sem2("in_experts"), sem2("in_last")
        s_clear, s_zero = sem("s_clear"), sem("s_zero")
        s_braw, s_bsplit, s_bdram, s_sel = (sem(n) for n in ("s_braw", "s_bsplit", "s_bdram", "s_sel"))
        s_dve = sem("dve_chain")
        s_embed = sem("s_embed")
        s_ve = [None if k == 3 else sem(f"s_ve_{k}") for k in range(5)]
        s_rstd = [None if k == 3 else sem(f"s_rstd_{k}") for k in range(5)]
        s_xln = [sem(f"s_xln_{k}") for k in range(5)]
        s_tr = [sem(f"s_tr_{k}") for k in range(5)]
        s_xnT = [sem(f"s_xnT_{k}") for k in range(5)]
        s_qk, s_qkev, s_v, s_vev, s_vones, s_x3 = sem2("s_qk"), sem2("s_qkev"), sem("s_v"), sem2("s_vev"), sem2("s_vones"), sem("s_x3")
        s_kb = sem2("s_kb")
        s_vd, s_vdev, s_vout, in_v = sem("s_vd"), sem("s_vdev"), sem("s_vout"), sem2("in_v")
        s_scores, s_sadd, s_sub, s_exp = sem2("s_scores"), sem2("s_sadd"), sem2("s_sub"), sem2("s_exp")
        s_pt, s_ptev, s_pv, s_norm = sem2("s_pt"), sem2("s_ptev"), sem2("s_pv"), sem2("s_norm")
        s_ct, s_ctev, s_proj, s_hb = sem2("s_ct"), sem2("s_ctev"), sem2("s_proj"), sem2("s_hb")
        s_logit, s_z, s_sig, s_mask, s_rank, s_onehot, s_found, s_index, s_slots = (
            sem2(n) for n in ("s_logit", "s_z", "s_sig", "s_mask", "s_rank", "s_onehot", "s_found", "s_index", "s_slots"))
        s_shup, s_shact, s_shdown, s_shev, s_hb2 = (sem(n) for n in ("s_shup", "s_shact", "s_shdown", "s_shev", "s_hb2"))
        s_xn = sem2("s_xn")
        s_col, s_onehot_pool = sem2("s_col"), sem2("s_onehot_pool")
        s_xb = [sem2(f"s_xb{L}") for L in range(2)]
        s_acc, s_add, s_added = sem2("s_acc"), sem2("s_add"), sem("s_added")
        s_xtr, s_xtev, s_up, s_silu, s_act = sem2("s_xtr"), sem2("s_xtev"), sem2("s_up"), sem2("s_silu"), sem2("s_act")
        s_atr, s_atev, s_down, s_yev = sem2("s_atr"), sem2("s_atev"), sem2("s_down"), sem2("s_yev")
        s_back = [sem(f"s_back_{t}") for t in range(NT)]
        s_pad = sem("s_pad")

        def block_steps(L, eng, first, step):
            first()
            step(0, 0, 0)
            step(1, 1, 1)
            turns = (ALWAYS - 3) // 2
            with eng.Fori(1, turns + 1) as i:
                step(i * 2, 0, 2)
                step(i * 2 + 1, 1, 3)
            for b in range(2 * turns + 2, ALWAYS - 1):
                step(b, b % 2, b)
            eng.wait_ge(s_slots[L], 1)
            used = eng.to_reg(eng.value_load(be_i[0:1, BLOCKS_USED:BLOCKS_USED + 1], min_val=ALWAYS,
                                             max_val=BLOCKS[L]))
            for b in range(ALWAYS - 1, BLOCKS[L]):
                if b < BLOCKS[L] - 1:
                    with eng.If_cmp(used, b + 1, 'IS_GT'):
                        step(b, b % 2, b)
                with eng.If_eq(used, b + 1):
                    step(b, b % 2, BLOCKS[L] - 1)

        block = ctx.enter_context(nc.Block())

        @block.sync
        def _(sp):
            for k in range(6):
                sp.dma_start(patch[:, k, :], a["patches"][:, k, :]).then_inc(in_patch[k], 16)
                sp.dma_start(tokw[:, k, :], a["tok_w"][:, k, :]).then_inc(in_patch[k], 16)
            sp.dma_start(cst[:, :], a["consts"]).then_inc(in_const, 16)
            sp.dma_start(wA[:, 0:256], a["wq0"]).then_inc(in_attn[0], 16)
            sp.dma_start(wA[:, 512:768], a["wk0"]).then_inc(in_attn[0], 16)
            sp.dma_start(wA[:, 1024:1152], a["wv0"]).then_inc(in_attn[0], 16)
            sp.dma_start(wA[:, 1536:2048], a["wo0"]).then_inc(in_attn[0], 16)
            sp.dma_start(bp, a["bp"].partition_broadcast(P)).then_inc(in_small, 16)
            sp.dma_start(sbd, a["sbd"].partition_broadcast(P)).then_inc(in_small, 16)
            sp.dma_start(sbu, a["sbu"]).then_inc(in_small, 16)
            sp.dma_start(gb, a["gamma_beta"]).then_inc(in_small, 16)
            sp.dma_start(braw, a["biases"]).then_inc(s_braw, 16)
            sp.dma_start(selraw, a["select"]).then_inc(s_braw, 16)
            sp.dma_start(gateT[:, :, 0:8], a["gate0"]).then_inc(in_small, 16)
            sp.dma_start(gbias[:, 0:8], a["gbias0"].partition_broadcast(P)).then_inc(in_small, 16)
            sp.dma_start(abias[:, :], a["attn_bias0"]).then_inc(in_attn[0], 16)
            sp.wait_ge(s_clear, 1)
            for L in range(2):
                sp.dma_start(a["sums"][L][TOK:TOK + P, :], zeros).then_inc(s_zero, 16)
            sp.wait_ge(s_bsplit, 3)
            for i in range(3):
                sp.dma_start(a["bias_parts"][i].rearrange("(p n) -> p n", p=P), bparts[i]).then_inc(s_bdram, 16)
            sp.dma_start(slot(0, 0, 4096), a["experts0"][0]).then_inc(in_shared, 16)
            for s in range(1, 7):
                sp.dma_start(slot(s, 0, 4096), a["experts0"][s]).then_inc(in_experts[0], 16)
            sp.wait_ge(s_bdram, 48)

            def place_biases(e0, e1):
                wb = W[:, :].bitcast(BF16)
                spare = dims(wb[0:9, :], 9, 2 * SLOT)
                for seg in range(3):
                    src = a["bias_parts"].rearrange("j (e s n) -> s j e n", e=8, s=3)[seg, :, e0:e1, :]
                    sp.dma_start(spare[3 * seg:3 * seg + 3, 1 + e0:1 + e1, 8192:8704], src).then_inc(in_bias, 16)

            place_biases(0, 6)
            sp.wait_ge(s_pv[0], PAIRS)
            for s in range(7, 9):
                sp.dma_start(slot(s, 0, 4096), a["experts0"][s]).then_inc(in_last[0], 16)
            place_biases(6, 8)
            sp.wait_ge(s_proj[0], NT)
            sp.dma_start(wA[:, 0:512], a["wq1"]).then_inc(in_attn[1], 16)
            sp.dma_start(wA[:, 512:1024], a["wk1"]).then_inc(in_attn[1], 16)
            sp.dma_start(wA[:, 1024:1536], a["wv1"]).then_inc(in_attn[1], 16)
            sp.dma_start(wA[:, 1536:2048], a["wo1"]).then_inc(in_attn[1], 16)

            def load_expert(s):
                sp.dma_start(slot(s, 0, SLOT), a["experts1"][s]).then_inc(in_experts[1], 16)

            def rows(L):
                k_ln = 4 if L else 1
                for t in range(NT):
                    sp.wait_ge(s_xln[k_ln], t + 1)
                    sp.dma_start(a["xn"][L][t * P:t * P + ROWS[t], :], xln[0:ROWS[t], t, :]).then_inc(s_xn[L], 16)
                sp.wait_ge(*((s_ve[4], NT) if L else (s_shev, NT)))
                for t in range(NT):
                    sp.dma_start(a["sums"][L][t * P:t * P + ROWS[t], :], h[0:ROWS[t], t, :]).then_inc(s_acc[L], 16)
                if L == 0:
                    sp.dma_start(abias[:, :], a["attn_bias1"]).then_inc(in_attn[1], 16)
                    load_expert(0)
                    sp.wait_ge(s_down[0], NT)
                    load_expert(1)

            rows(0)
            sp.wait_ge(s_added, 1)
            for t in range(NT):
                sp.dma_start(h[0:ROWS[t], t, :], a["sums"][0][t * P:t * P + ROWS[t], :]).then_inc(s_back[t], 16)
            load_expert(2)
            load_expert(3)
            sp.dma_start(gateT[:, :, :], a["gate1"]).then_inc(in_gate, 16)
            sp.dma_start(gbias[:, :], a["gbias1"].partition_broadcast(P)).then_inc(in_gate, 16)
            for t in range(NT):
                sp.wait_ge(s_vdev, t + 1)
                sp.dma_start(a["values"][t * P:t * P + ROWS[t], :], v_t[0:ROWS[t], t, :]).then_inc(s_vout, 16)
            sp.wait_ge(s_vout, 16 * NT)
            for q in range(4):
                if q >= 2:
                    sp.wait_ge(s_vev[1], q - 1)
                for c in range(3):
                    sp.dma_start(vraw[q % 2][PATCHES * c:PATCHES * (c + 1), :, :, :].rearrange("p i h d -> p i (h d)"),
                                 a["values"].rearrange("(i k) d -> k i d", k=PATCHES)[:, 4 * q:4 * q + 4, :]
                                 ).then_inc(in_v[q % 2], 16)
            for s in range(4, 7):
                load_expert(s)
            sp.wait_ge(s_pv[1], PAIRS)
            for s in range(7, 9):
                sp.dma_start(slot(s, 0, SLOT), a["experts1"][s]).then_inc(in_last[1], 16)
            rows(1)

        @block.gpsimd
        def _(g):
            def power(k):
                n = 2 if k == 2 else 1
                for t in range(NT):
                    g.wait_ge(s_ve[k], t + 1)
                    nc.gpsimd.tensor_tensor(rstd[:, t, 0:n], ve[:, t, 0:n], mhalf[:, 0:n], ALU.pow).then_inc(s_rstd[k], 1)

            def key_blocks(L):
                km = dims(const(f"kmask{L}"), 2, HB)
                for p in range(PAIRS):
                    if p % 4 == 0:
                        g.wait_ge(s_qkev[L], (1 + p // 4) * 2 * CH[L])
                    if p >= 2:
                        g.wait_ge(s_scores[L], p - 1)
                    for u in range(2):
                        keys = dims(kT[:, u if L else 0, 72 * p:72 * (p + 1)], 2, PATCHES)
                        nc.gpsimd.tensor_tensor(
                            kb[p % 2][:, u, :, :].rearrange("p i (h k) -> p i h k", h=HB),
                            keys.unsqueeze(2).broadcast_to([P, 2, HB, PATCHES]),
                            km[:, u, :].unsqueeze(1).unsqueeze(3).broadcast_to([P, 2, HB, PATCHES]),
                            ALU.mult).then_inc(s_kb[L], 1)

            def onehots(L):
                g.wait_ge(s_col[L], 1)
                for j in range(DVE_COLS, 2 * NT):
                    last = nc.gpsimd.tensor_scalar(onehot[L][:, j, :], const("iota"), rt[:, 440 + j:441 + j], None,
                                                   ALU.is_equal)
                last.then_inc(s_onehot_pool[L], 1)

            def move_blocks(L):
                def gather(b):
                    if b >= 2:
                        g.wait_ge(s_xtr[L], b - 1)
                    g.indirect_dma_start(
                        xb[b % 2], None, a["xn"][L],
                        bass.IndirectOffsetOnAxis(gather_i[:, b:b + 1].bitcast(U32), 0)).then_inc(s_xb[L][b % 2], 16)

                def add(b):
                    g.wait_ge(s_yev[L], b + 1)
                    if b >= 1:
                        g.wait_ge(s_add[L], 16 * b)
                    g.indirect_dma_start(
                        a["sums"][L], bass.IndirectOffsetOnAxis(add_i[:, b:b + 1].bitcast(U32), 0),
                        ys[b % 2], None, compute_op=ALU.add).then_inc(s_add[L], 16)

                g.wait_ge(s_xn[L], 16 * NT)
                g.wait_ge(s_index[L], 1)
                gather(0)
                gather(1)
                gather(2)
                g.wait_ge(s_index[L], 2)
                g.wait_ge(s_acc[L], 16 * NT)
                g.wait_ge(s_slots[L], 1)
                used = g.to_reg(g.value_load(be_i[0:1, BLOCKS_USED:BLOCKS_USED + 1], min_val=ALWAYS,
                                             max_val=BLOCKS[L]))
                for b in range(BLOCKS[L]):
                    if b + 3 <= ALWAYS:
                        gather(b + 3)
                    elif b + 3 < BLOCKS[L]:
                        with g.If_cmp(used, b + 2, 'IS_GT'):
                            gather(b + 3)
                    if b < ALWAYS:
                        add(b)
                    else:
                        with g.If_cmp(used, b, 'IS_GT'):
                            add(b)
                g.wait_ge(s_add[L], 16 * ALWAYS)
                for b in range(ALWAYS, BLOCKS[L]):
                    with g.If_cmp(used, b, 'IS_GT'):
                        g.wait_ge(s_add[L], 16 * (b + 1))

            g.wait_ge(s_clear, 1)
            power(0)
            g.wait_ge(s_xln[0], NT)
            g.wait_ge(in_small, 96)
            nc.gpsimd.tensor_tensor(h, h, bp.unsqueeze(1).broadcast_to([P, NT, D]), ALU.add).then_inc(s_hb[0], 1)
            g.wait_ge(in_const, 16)
            key_blocks(0)
            power(1)
            nc.gpsimd.tensor_scalar(sbd, sbd, 0.1, None, ALU.mult).then_inc(s_hb2, 1)
            g.wait_ge(s_hb2, 1)
            g.wait_ge(s_xln[1], NT)
            nc.gpsimd.tensor_tensor(h, h, sbd.unsqueeze(1).broadcast_to([P, NT, D]), ALU.add).then_inc(s_hb2, 1)
            def load_expert(s):
                g.dma_start(slot(s, 0, SLOT), a["experts1"][s]).then_inc(in_experts[1], 16)

            onehots(0)
            move_blocks(0)
            g.sem_inc(s_added, 1)
            power(2)
            g.wait_ge(s_xln[2], NT)
            nc.gpsimd.tensor_tensor(h, h, xln, ALU.add).then_inc(s_hb[1], 1)
            key_blocks(1)
            power(4)
            onehots(1)
            move_blocks(1)

        @block.tensor
        def _(pe):
            mm = nc.tensor.matmul

            def transposes_ln(k, src, gate=None):
                for t in range(NT + 1):
                    if t < NT:
                        n = ROWS[t]
                        pe.wait_ge(s_xln[k], t + 1)
                        if t >= 2:
                            pe.wait_ge(s_xnT[k], t - 1)
                        for c in range(2):
                            last = nc.tensor.transpose(PS[:, LN_BANK[t % 2], c * P:c * P + n],
                                                       src[0:n, t, c * P:(c + 1) * P], ident[0:n, 0:n])
                        last.then_inc(s_tr[k], 1)
                    if gate is not None and t >= 1:
                        logits(gate, k, t - 1)

            def logits(L, k_ln, t):
                if t == 0:
                    pe.wait_ge(*((in_gate, 32) if L else (in_small, 96)))
                pe.wait_ge(s_xnT[k_ln], t + 1)
                n, E = ROWS[t], EXPERTS[L]
                for k in range(2):
                    last = mm(PS[0:n, 6, E * t:E * (t + 1)], xnT[:, k, t * P:t * P + n],
                              gateT[:, k, 0:E], start=(k == 0), stop=(k == 1))
                last.then_inc(s_logit[L], 1)

            def attention(L, k_ln):
                dq = DQ[L]
                pe.wait_ge(in_attn[L], 80)
                pe.wait_ge(s_xnT[k_ln], NT)
                if L == 1:
                    for t in range(NT):
                        n = ROWS[t]
                        if t >= 3:
                            pe.wait_ge(s_vdev, t - 2)
                        for k in range(2):
                            last = mm(PS[0:n, V_BANK[t % 3], 0:D], xnT[:, k, t * P:t * P + n], wv[1][:, k, :],
                                      start=(k == 0), stop=(k == 1))
                        last.then_inc(s_vd, 1)
                items = [(w[L], c, i) for i in range(2) for w in (wq, wk) for c in range(CH[L])]
                for i, (w, c, half) in enumerate(items):
                    if i >= 4:
                        pe.wait_ge(s_qkev[L], i - 3)
                    for k in range(2):
                        last = mm(PS[:, i % 4, 0:HALF], w[:, k, c * P:(c + 1) * P],
                                  xnT[:, k, half * HALF:(half + 1) * HALF], start=(k == 0), stop=(k == 1))
                    last.then_inc(s_qk[L], 1)

                def scores(p):
                    pe.wait_ge(s_kb[L], 2 * (p + 1))
                    if p >= 2:
                        pe.wait_ge(s_sadd[L], p - 1)
                    else:
                        pe.wait_ge(s_qkev[L], len(items))
                    for u in range(2):
                        for par in range(2):
                            at = (2 * p + par) * PATCHES
                            last = mm(PS[64 * par:64 * par + PATCHES, 2 * (p % 2) + u, 0:HB * PATCHES],
                                      qT[:, u if L else 0, at:at + PATCHES], kb[p % 2][:, u, par, :],
                                      start=True, stop=True)
                    last.then_inc(s_scores[L], 1)

                if L == 1:
                    scores(0)
                    scores(1)
                else:
                    pe.wait_ge(s_x3, 2)
                for i in range(0 if L else IMGS):
                    if i >= 3:
                        pe.wait_ge(s_vev[L], i - 2)
                    for k in range(2):
                        last = mm(PS[0:108, V_BANK[i % 3], 0:64],
                                  x3[k][:, i, :, :].rearrange("p r q -> p (r q)"), wv[L][:, k, :],
                                  start=(k == 0), stop=(k == 1))
                    last.then_inc(s_v, 1)
                    if i in EARLY:
                        scores(EARLY.index(i))

                def prob_turn(p):
                    pe.wait_ge(s_exp[L], p + 1)
                    if p >= 1:
                        pe.wait_ge(s_ptev[L], 2 * p)
                    else:
                        pe.wait_ge(*((s_vdev, NT) if L else (s_vev[0], IMGS)))
                    for g, (h0, nh) in enumerate(GROUPS):
                        last = nc.tensor.transpose(
                            ps_flat[0:nh * PATCHES, 4 * 512 + g * P:4 * 512 + (g + 1) * P],
                            prob[p % 2][:, h0 * PATCHES:(h0 + nh) * PATCHES], ident)
                    last.then_inc(s_pt[L], 1)

                def values(p):
                    pe.wait_ge(s_ptev[L], 2 * (p + 1))
                    if p >= 1:
                        pe.wait_ge(s_norm[L], p)
                    else:
                        pe.wait_ge(s_vones[L], 2)
                    if L == 1 and p % 2 == 0:
                        pe.wait_ge(s_vev[L], p // 2 + 1)
                    elif p == 0:
                        pe.wait_ge(s_vev[L], IMGS)
                    for par in range(2):
                        for g, (h0, nh) in enumerate(GROUPS):
                            k = nh * PATCHES
                            last = mm(PS[64 * par:64 * par + PATCHES, 6, h0 * VW:(h0 + nh) * VW],
                                      pT[p % 2][0:k, g, par * PATCHES:(par + 1) * PATCHES],
                                      vblk[0:k, 2 * p + par, h0:h0 + nh, :], start=True, stop=True)
                    last.then_inc(s_pv[L], 1)

                def ctx_turn(p):
                    pe.wait_ge(s_norm[L], p + 1)
                    if p >= 1:
                        pe.wait_ge(s_ctev[L], p)
                    for c in range(2):
                        last = nc.tensor.transpose(PS[:, 7, c * P:(c + 1) * P],
                                                   ctxn[p % 2][:, c * P:(c + 1) * P], ident)
                    last.then_inc(s_ct[L], 1)

                def project(t):
                    n = ROWS[t]
                    pe.wait_ge(s_ctev[L], -(-(t * P + n) // (2 * PATCHES)))
                    if t < 4:
                        pe.wait_ge(s_sadd[L], PAIRS - 1 + t // 2)
                    for k in range(2):
                        last = mm(PS[0:n, t, 0:D], ctxT[:, k, t * P:t * P + n], wo[:, k, :],
                                  start=(k == 0), stop=(k == 1))
                    last.then_inc(s_proj[L], 1)

                for i in range(PAIRS + 1):
                    if i < PAIRS:
                        prob_turn(i)
                    if i < PAIRS - 2:
                        scores(i + 2)
                    if i >= 1:
                        ctx_turn(i - 1)
                    if i < PAIRS:
                        values(i)
                    if i == PAIRS - 1:
                        project(0)
                        project(1)
                project(2)
                project(3)
                project(4)

            def ranks(L):
                E = EXPERTS[L]
                pe.wait_ge(s_mask[L], 1)
                mm(PS[:, 6, 0:(NT + 1) * E], tri_b[:, :], mask_b[:, :, 0:E], start=True, stop=False)
                for u in range(NT):
                    last = mm(PS[:, 6, (u + 1) * E:(NT + 1) * E], ones_b[:, :],
                              mask_b[:, u:u + 1, 0:E].broadcast_to([P, NT - u, E]), start=False, stop=(u == NT - 1))
                last.then_inc(s_rank[L], 1)

            def turn_places(L):
                for i, (v0, v1) in enumerate(TURNS[L]):
                    c0, c1 = v0 * BLOCKS[L], v1 * BLOCKS[L]
                    pe.wait_ge(s_onehot[L], i + 1)
                    for j in range(2 * NT):
                        if i == 0 and j == DVE_COLS:
                            pe.wait_ge(s_onehot_pool[L], 1)
                        n = ROWS[j % NT]
                        last = mm(PS[:, 6, c0:c1], onehot[L][0:n, j, :], place_vals[0:n, j, c0:c1],
                                  start=(j == 0), stop=(j == 2 * NT - 1))
                    last.then_inc(s_found[L], 1)

            def shared_up():
                pe.wait_ge(in_shared, 16)
                for i in range(16):
                    c, half = i // 2, i % 2
                    if i >= 4:
                        pe.wait_ge(s_shact, i - 3)
                    for k in range(2):
                        last = mm(PS[:, i % 4, 0:HALF], slot(0, k * 1024 + c * P, P),
                                  xnT[:, k, half * HALF:(half + 1) * HALF], start=(k == 0), stop=(k == 1))
                    last.then_inc(s_shup, 1)

            def shared_down():
                pe.wait_ge(s_shact, 16)
                for t in range(NT):
                    n = ROWS[t]
                    if t == 3:
                        turn_places(0)
                    if t == NT - 1:
                        turn_first_rows(0)
                    for f in range(8):
                        last = mm(PS[0:n, SH_BANK[t], 0:D], shT[:, f, t * P:t * P + n],
                                  slot(0, 2048 + f * D, D), start=(f == 0), stop=(f == 7))
                    last.then_inc(s_shdown, 1)

            def rows_turn(L, b, par, k):
                pe.wait_ge(s_xb[L][par], (b // 2 + 1) * 16 if isinstance(b, int) else (b - par) * 8 + 16)
                if k >= 1:
                    pe.wait_ge(s_xtev[L], b)
                for c in range(2):
                    last = nc.tensor.transpose(PS[:, 7, c * P:(c + 1) * P],
                                               xb[par][:, c * P:(c + 1) * P], ident)
                last.then_inc(s_xtr[L], 1)

            def turn_first_rows(L):
                rows_turn(L, 0, 0, 0)
                rows_turn(L, 1, 1, 1)

            def experts(L):
                seg = SEG[L]
                wb = W[:, :].bitcast(BF16)

                def expert_of(b):
                    return pe.value_load(be_i[0:1, bass.ds(b, 1)], min_val=0, max_val=8)

                def up(b, par, k, s, e):
                    pe.wait_ge(s_xtev[L], b + 1)
                    if k >= 1:
                        pe.wait_ge(s_act[L], 2 * b + s - 1)
                    if k == 0 and L == 0 and s == 1:
                        pe.wait_ge(s_shev, NT)
                    for part in range(L + 1):
                        bank = s + 2 * part
                        for c in range(2):
                            off = e * SLOT + part * 2 * HID[L] + c * HID[L] + s * seg
                            last = mm(PS[:, bank, 0:seg], xbT[par][:, c, :], W[:, bass.ds(off, seg)],
                                      start=(c == 0), stop=(L == 1 and c == 1))
                        if L == 0:
                            last = mm(PS[:, bank, 0:seg], sel[:, s, :], wb[0:9, bass.ds(e * 2 * SLOT + 8192, seg)],
                                      start=False, stop=True)
                    last.then_inc(s_up[L], 1)

                def act_turn(b, par, k):
                    pe.wait_ge(s_act[L], 2 * b + 2)
                    if k >= 1:
                        pe.wait_ge(s_atev[L], 2 * b)
                    elif L == 0:
                        pe.wait_ge(s_shev, NT)
                    for f in range(FCH[L]):
                        last = nc.tensor.transpose(ps_flat[:, 4 * 512 + f * P:4 * 512 + (f + 1) * P],
                                                   act[par][:, f * P:(f + 1) * P], ident)
                        if f in (3, FCH[L] - 1):
                            last.then_inc(s_atr[L], 1)

                def down(b, par, k, e):
                    pe.wait_ge(s_atev[L], 2 * b + 2)
                    if k >= 1:
                        pe.wait_ge(s_yev[L], b)
                    base = 2 * HID[L] * (L + 1)
                    y = PS[:, 6, 0:D]
                    for f in range(FCH[L]):
                        last = mm(y, actT[:, f * P:(f + 1) * P], W[:, bass.ds(e * SLOT + base + f * D, D)],
                                  start=(f == 0), stop=(L == 1 and f == FCH[L] - 1))
                    if L == 0:
                        last = mm(y, sel[:, 2, :], wb[0:9, bass.ds(e * 2 * SLOT + 8192, D)], start=False, stop=True)
                    last.then_inc(s_down[L], 1)

                def step(b, par, k):
                    more = k < BLOCKS[L] - 1
                    if more:
                        e1 = expert_of(b + 1)
                        up(b + 1, 1 - par, 1, 0, e1)
                    act_turn(b, par, k)
                    if more:
                        up(b + 1, 1 - par, 1, 1, e1)
                    if k < BLOCKS[L] - 2:
                        rows_turn(L, b + 2, par, 2)
                    down(b, par, k, expert_of(b))
                    if not more:
                        pe.wait_ge(s_xtev[L], min(b + 2, BLOCKS[L]))

                def first():
                    pe.wait_ge(s_slots[L], 1)
                    if L == 1:
                        turn_first_rows(1)
                    pe.wait_ge(in_experts[L], 16 * (6 + L))
                    pe.wait_ge(in_last[L], 32)
                    if L == 0:
                        pe.wait_ge(in_bias, 16 * 6)
                        pe.wait_ge(s_sel, 1)
                    e0 = expert_of(0)
                    up(0, 0, 0, 0, e0)
                    up(0, 0, 0, 1, e0)

                block_steps(L, pe, first, step)

            for k in range(6):
                pe.wait_ge(in_patch[k], 32)
                for t in range(NT):
                    n = ROWS[t]
                    last = mm(PS[0:n, t, 0:D], patch[:, k, t * P:t * P + n], tokw[:, k, :],
                              start=(k == 0), stop=(k == 5))
                    if k == 5:
                        last.then_inc(s_embed, 1)
            pe.wait_ge(in_const, 16)
            transposes_ln(0, xln)
            attention(0, 0)
            transposes_ln(1, xln, gate=0)
            shared_up()
            ranks(0)
            shared_down()
            experts(0)
            transposes_ln(3, xln2)
            attention(1, 3)
            transposes_ln(4, xln, gate=1)
            ranks(1)
            turn_places(1)
            experts(1)

        @block.scalar
        def _(ac):
            def copies_ln(k, affine=False):
                for t in range(NT):
                    n = ROWS[t]
                    ac.wait_ge(s_tr[k], t + 1)
                    src = dims(PS[:, LN_BANK[t % 2], 0:256], 2, P)[:, :, 0:n]
                    if not affine:
                        nc.scalar.copy(xnT[:, :, t * P:t * P + n], src).then_inc(s_xnT[k], 1)
                        continue
                    nc.scalar.activation(xnT[:, 0, t * P:t * P + n], src[:, 0, :], ACT.Identity,
                                         bias=gb[:, 2:3], scale=gb[:, 0:1])
                    nc.scalar.activation(xnT[:, 1, t * P:t * P + n], src[:, 1, :], ACT.Identity,
                                         bias=gb[:, 3:4], scale=gb[:, 1:2]).then_inc(s_xnT[k], 1)

            def attention(L, k_ln):
                if L == 0:
                    ac.wait_ge(s_xnT[k_ln], NT)
                    nc.scalar.copy(x3[1], dims(xnT[:, 1, :], IMGS, PATCHES).unsqueeze(2).broadcast_to(
                        [P, IMGS, 3, PATCHES])).then_inc(s_x3, 1)
                for i in range(4 * CH[L]):
                    ac.wait_ge(s_qk[L], i + 1)
                    half, c = i // (2 * CH[L]), i % CH[L]
                    part = slice(half * HALF, (half + 1) * HALF)
                    if i // CH[L] % 2 == 0:
                        nc.scalar.mul(qT[:, c, part], PS[:, i % 4, 0:HALF], QSCALE[L]).then_inc(s_qkev[L], 1)
                    else:
                        if L == 0 and i == 1:
                            ac.wait_ge(s_bdram, 48)
                            ac.wait_ge(s_sel, 1)
                        nc.scalar.copy(kT[:, c, part], PS[:, i % 4, 0:HALF]).then_inc(s_qkev[L], 1)

                def exp(p):
                    ac.wait_ge(s_sub[L], p + 1)
                    nc.scalar.activation(prob[p % 2], prob[p % 2], ACT.Exp).then_inc(s_exp[L], 1)

                def prob_out(p):
                    ac.wait_ge(s_pt[L], p + 1)
                    if p >= 2:
                        ac.wait_ge(s_pv[L], p - 1)
                    src = dims(ps_flat[:, 4 * 512:4 * 512 + 6 * P], 6, 2, 64)
                    for g0, g1, k in ((0, 5, 108), (5, 6, PATCHES)):
                        dst = pT[p % 2][0:k, g0:g1, :].rearrange("p g (i q) -> p g i q", i=2)
                        nc.scalar.copy(dst, src[0:k, g0:g1, :, 0:PATCHES]).then_inc(s_ptev[L], 1)

                def ctx_out(p):
                    ac.wait_ge(s_ct[L], p + 1)
                    src = dims(PS[:, 7, 0:256], 2, 2, 64)[:, :, :, 0:PATCHES]
                    dst = ctxT[:, :, 72 * p:72 * (p + 1)].rearrange("p c (i q) -> p c i q", i=2)
                    nc.scalar.copy(dst, src).then_inc(s_ctev[L], 1)

                exp(0)
                for i in range(PAIRS + 1):
                    if i < PAIRS - 1:
                        exp(i + 1)
                    if i < PAIRS:
                        prob_out(i)
                    if i >= 1:
                        ctx_out(i - 1)

            def sigmoid(L):
                E = EXPERTS[L]
                ac.wait_ge(s_z[L], 1)
                nc.scalar.activation(rt[:, 2 * 45:2 * 45 + NT * E], rt[:, 45:45 + NT * E],
                                     ACT.Sigmoid).then_inc(s_sig[L], 1)

            def experts(L):
                seg = SEG[L]

                def rows_copy(b, par, k):
                    ac.wait_ge(s_xtr[L], b + 1)
                    if k >= 2:
                        ac.wait_ge(s_up[L], 2 * b - 2)
                    nc.scalar.copy(xbT[par], dims(PS[:, 7, 0:256], 2, P)
                                   ).then_inc(s_xtev[L], 1)

                def gate(b, par, k, s):
                    ac.wait_ge(s_up[L], 2 * b + s + 1)
                    if k >= 2:
                        ac.wait_ge(s_atr[L], 2 * b - 2)
                    nc.scalar.activation(act[par][:, s * seg:(s + 1) * seg], PS[:, s, 0:seg],
                                         ACT.Silu if L else ACT.Gelu).then_inc((s_silu if L else s_act)[L], 1)

                def step(b, par, k):
                    if k < BLOCKS[L] - 1:
                        gate(b + 1, 1 - par, k + 1, 0)
                        gate(b + 1, 1 - par, k + 1, 1)
                    if k < BLOCKS[L] - 2:
                        rows_copy(b + 2, par, 2)

                def first():
                    rows_copy(0, 0, 0)
                    rows_copy(1, 1, 1)
                    if L == 1:
                        ac.wait_ge(s_pad, 1)
                    gate(0, 0, 0, 0)
                    gate(0, 0, 0, 1)

                block_steps(L, ac, first, step)

            copies_ln(0)
            attention(0, 0)
            copies_ln(1)
            sigmoid(0)
            ac.wait_ge(in_small, 96)
            for i in range(16):
                c, half = i // 2, i % 2
                ac.wait_ge(s_shup, i + 1)
                nc.scalar.activation(shT[:, c, half * HALF:(half + 1) * HALF], PS[:, i % 4, 0:HALF],
                                     ACT.Gelu, bias=sbu[:, c:c + 1]).then_inc(s_shact, 1)
            experts(0)
            copies_ln(3, affine=True)
            attention(1, 3)
            copies_ln(4)
            sigmoid(1)
            experts(1)

        @block.vector
        def _(v):
            chained = [0]

            def link(ins):
                chained[0] += 1
                ins.then_inc(s_dve, 1)
                v.wait_ge(s_dve, chained[0])

            TT, TS, STT = nc.vector.tensor_tensor, nc.vector.tensor_scalar, nc.vector.scalar_tensor_tensor

            def done(ins):
                ins.then_inc(s_dve, 1)
                chained[0] += 1
                return chained[0]

            def layernorm(k, tile_in):
                n1, n2, n3 = [0] * NT, [0] * NT, [0] * NT
                for i in range(NT + LAG):
                    if i >= LAG:
                        t = i - LAG
                        v.wait_ge(s_rstd[k], t + 1)
                        dst, which, out_k = (xln2, 1, 3) if k == 2 else (xln, 0, k)
                        TS(dst[:, t, :], h[:, t, :], mv[:, t, 0:1], rstd[:, t, which:which + 1], ALU.subtract,
                           ALU.mult).then_inc(s_xln[out_k], 1)
                    if 3 <= i <= NT + 2:
                        t = i - 3
                        v.wait_ge(s_dve, n3[t])
                        if k == 2:
                            TS(ve[:, t, 1:2], mv[:, t, 1:2], 1.0 + EPS_LN, EPS_LN * EPS_LN, ALU.mult, ALU.add)
                        TS(ve[:, t, 0:1], mv[:, t, 1:2], EPS_LN, None, ALU.add).then_inc(s_ve[k], 1)
                    if 2 <= i <= NT + 1:
                        t = i - 2
                        v.wait_ge(s_dve, n2[t])
                        n3[t] = done(nc.vector.bn_aggr(mv[:, t, :], stats[:, t, :]))
                    if 1 <= i <= NT:
                        t = i - 1
                        if n1[t]:
                            v.wait_ge(s_dve, n1[t])
                        n2[t] = done(nc.vector.bn_stats(stats[:, t, :], h[:, t, :]))
                    if i < NT:
                        n1[i] = done(tile_in(i)) if k != 2 else tile_in(i)
                if k == 2:
                    for t in range(NT):
                        TS(xln[:, t, :], h[:, t, :], mv[:, t, 0:1], rstd[:, t, 0:1], ALU.subtract,
                           ALU.mult).then_inc(s_xln[k], 1)

            def attention(L, k_ln):
                mask = const("vmask")[0:108, :]
                v.wait_ge(s_xnT[k_ln], NT)
                if L == 0:
                    nc.vector.tensor_copy(x3[0], dims(xnT[:, 0, :], IMGS, PATCHES).unsqueeze(2).broadcast_to(
                        [P, IMGS, 3, PATCHES])).then_inc(s_x3, 1)
                else:
                    for t in range(NT):
                        n = ROWS[t]
                        v.wait_ge(s_vd, t + 1)
                        nc.vector.tensor_copy(v_t[0:n, t, :], PS[0:n, V_BANK[t % 3], 0:D]).then_inc(s_vdev, 1)
                def softmax(p):
                    t = prob[p % 2]
                    v.wait_ge(s_scores[L], p + 1)
                    if p == 0:
                        v.wait_ge(in_attn[L], 80)
                        v.wait_ge(s_hb[L], 1)
                    if p >= 2:
                        v.wait_ge(s_pt[L], p - 1)
                    TT(dims(t, 2, HB * PATCHES), PS[:, 2 * (p % 2):2 * (p % 2) + 2, 0:HB * PATCHES],
                       dims(abias[:, :], 2, HB * PATCHES), ALU.add).then_inc(s_sadd[L], 1)
                    v.wait_ge(s_sadd[L], p + 1)
                    link(nc.vector.tensor_reduce(nmax, dims(t, HEADS, PATCHES), AX, ALU.max))
                    TT(dims(t, HEADS, PATCHES), dims(t, HEADS, PATCHES),
                       nmax.unsqueeze(2).broadcast_to([P, HEADS, PATCHES]), ALU.subtract).then_inc(s_sub[L], 1)

                nc.vector.tensor_copy(vblk[0:108, :, :, DH],
                                      mask.unsqueeze(1).broadcast_to([108, IMGS, HEADS])).then_inc(s_vones[L], 1)
                nc.vector.memset(PS[:, 6, 0:HEADS * VW], 1.0).then_inc(s_vones[L], 1)
                if L == 0:
                    for i in range(IMGS):
                        v.wait_ge(s_v, i + 1)
                        dst = vblk[0:108, i, :, 0:DH].rearrange("p (j c) d -> p j c d", j=4)
                        src = dims(PS[0:108, V_BANK[i % 3], 0:64], 4, DH).unsqueeze(1).broadcast_to([108, 4, 4, DH])
                        m = dims(mask, 4, 4).unsqueeze(3).broadcast_to([108, 4, 4, DH])
                        TT(dst, src, m, ALU.mult).then_inc(s_vev[L], 1)
                        if i in EARLY:
                            softmax(EARLY.index(i))
                else:
                    for q in range(4):
                        v.wait_ge(in_v[q % 2], 48 * (q // 2 + 1))
                        TT(vblk[0:108, 4 * q:4 * q + 4, :, 0:DH], vraw[q % 2],
                           mask.unsqueeze(1).unsqueeze(3).broadcast_to([108, 4, HEADS, DH]), ALU.mult
                           ).then_inc(s_vev[L], 1)
                        if q == 1:
                            softmax(0)
                            softmax(1)

                def normalize(p):
                    v.wait_ge(s_pv[L], p + 1)
                    link(nc.vector.reciprocal(rinv, ctx_ps[:, :, DH]))
                    if p >= 2:
                        v.wait_ge(s_ct[L], p - 1)
                    elif L == 0:
                        v.wait_ge(s_zero, 32)
                    TT(dims(ctxn[p % 2], HEADS, DH), ctx_ps[:, :, 0:DH],
                       rinv.unsqueeze(2).broadcast_to([P, HEADS, DH]), ALU.mult).then_inc(s_norm[L], 1)

                for i in range(PAIRS):
                    if i < PAIRS - 2:
                        softmax(i + 2)
                    normalize(i)

            def attn_out(L):
                def tile(t):
                    n = ROWS[t]
                    if t == 0:
                        v.wait_ge(s_hb[L], 1)
                    v.wait_ge(s_proj[L], t + 1)
                    return TT(h[0:n, t, :], PS[0:n, t, 0:D], h[0:n, t, :], ALU.add)
                return tile

            def route(L):
                E = EXPERTS[L]

                def tmp(i):
                    return dims(rt[:, 45 * i:45 * i + NT * E], NT, E)

                _, z, sig, key, oh1, oh2, t1, t2 = (tmp(i) for i in range(8))
                r5 = [rt[:, 360 + 5 * i:365 + 5 * i] for i in range(8)]
                nb, cum, start = (rt[:, 400 + 9 * i:400 + 9 * i + E] for i in range(3))
                ids, ids99 = (const(n)[:, 0:E].unsqueeze(1).broadcast_to([P, NT, E]) for n in ("ids", "ids99"))

                def bc(x):
                    return x.unsqueeze(2).broadcast_to([P, NT, E])

                v.wait_ge(s_logit[L], NT)
                TT(z, dims(PS[:, 6, 0:NT * E], NT, E), gbias[:, 0:E].unsqueeze(1).broadcast_to([P, NT, E]),
                   ALU.add).then_inc(s_z[L], 1)
                v.wait_ge(s_z[L], 1)
                link(TS(key, z, 17.0, -103.0, ALU.min, ALU.max))
                for oh, m, i in ((oh1, r5[0], r5[1]), (oh2, r5[2], r5[3])):
                    link(nc.vector.tensor_reduce(m, key, AX, ALU.max))
                    link(TT(t1, key, bc(m), ALU.is_equal))
                    link(STT(t1, t1, -99.0, ids, ALU.mult, ALU.add))
                    link(nc.vector.tensor_reduce(i, t1, AX, ALU.min))
                    link(TT(oh, ids99, bc(i), ALU.is_equal))
                    if oh is oh1:
                        link(STT(key, oh1, -1e6, key, ALU.mult, ALU.add))
                TT(mask_b[:, 0:NT - 1, 0:E], oh1[:, 0:NT - 1, :], oh2[:, 0:NT - 1, :], ALU.add)
                m = ROWS[NT - 1]
                TT(mask_b[0:m, NT - 1, 0:E], oh1[0:m, NT - 1, :], oh2[0:m, NT - 1, :], ALU.add).then_inc(s_mask[L], 1)
                v.wait_ge(s_sig[L], 1)
                TT(t1, sig, oh1, ALU.mult)
                link(TT(t2, sig, oh2, ALU.mult))
                nc.vector.tensor_reduce(r5[4], t1, AX, ALU.add)
                link(nc.vector.tensor_reduce(r5[5], t2, AX, ALU.add))

                def weights():
                    wf, rest = rt[:, 350:360], rt[:, 360:370]
                    link(STT(r5[2], r5[4], EPS_TOPK[L], r5[5], ALU.add, ALU.add))
                    link(nc.vector.reciprocal(r5[3], r5[2]))
                    TT(wf[:, 0:NT], r5[4], r5[3], ALU.mult)
                    link(TT(wf[:, NT:2 * NT], r5[5], r5[3], ALU.mult))
                    link(nc.vector.tensor_copy(vals_b[:, :, 3], wf))
                    link(TT(rest, wf, vals_b[:, :, 3], ALU.subtract))
                    link(nc.vector.tensor_copy(vals_b[:, :, 4], rest))
                    link(TT(rest, rest, vals_b[:, :, 4], ALU.subtract))
                    link(nc.vector.tensor_copy(vals_b[:, :, 5], rest))

                if L == 0:
                    weights()
                v.wait_ge(s_rank[L], 1)
                c5 = dims(rt[:, 45:45 + NT * E], E, NT)
                link(TT(c5, PS[:, 6, NT * E:(NT + 1) * E].unsqueeze(2).broadcast_to([P, E, NT]),
                        const("thr").unsqueeze(1).broadcast_to([P, E, NT]), ALU.is_gt))
                link(nc.vector.tensor_reduce(nb, c5, AX, ALU.add))
                ee = dims(rt[:, 90:90 + E * E], E, E)
                link(TT(ee, nb.unsqueeze(1).broadcast_to([P, E, E]), dims(const(f"before{L}"), E, E), ALU.mult))
                link(nc.vector.tensor_reduce(start, ee, AX, ALU.add))
                place = tmp(1)
                link(TT(place, dims(PS[:, 6, 0:NT * E], NT, E),
                        start.unsqueeze(1).broadcast_to([P, NT, E]), ALU.add))
                TT(t1, place, oh1, ALU.mult)
                link(TT(t2, place, oh2, ALU.mult))
                nc.vector.tensor_reduce(r5[6], t1, AX, ALU.add)
                link(nc.vector.tensor_reduce(r5[7], t2, AX, ALU.add))
                nb_ = BLOCKS[L]
                pos, J = rt[:, 390:400], 2 * NT
                ge = dims(rt[:, 0:J * (nb_ + 1)], J, nb_ + 1)
                block_1h = dims(rt[:, 180:180 + J * nb_], J, nb_)
                count, col = rt[:, 430:440], rt[:, 440:450]
                link(TT(ge, pos.unsqueeze(2).broadcast_to([P, J, nb_ + 1]),
                        const("edge")[:, 0:nb_ + 1].unsqueeze(1).broadcast_to([P, J, nb_ + 1]), ALU.is_ge))
                TT(block_1h, ge[:, :, 0:nb_], ge[:, :, 1:nb_ + 1], ALU.subtract)
                link(nc.vector.tensor_reduce(count, ge, AX, ALU.add))
                STT(col, count, -float(P), pos, ALU.mult, ALU.add).then_inc(s_col[L], 1)
                v.wait_ge(s_col[L], 1)

                def spread(v0, v1):
                    m = v1 - v0
                    return TT(place_vals[:, :, v0 * nb_:v1 * nb_].rearrange("p j (v b) -> p j v b", v=m),
                              block_1h.unsqueeze(2).broadcast_to([P, J, m, nb_]),
                              vals_b[:, :, v0:v1].unsqueeze(3).broadcast_to([P, J, m, nb_]), ALU.mult)

                spread(*TURNS[L][0])
                for j in range(DVE_COLS):
                    last = TS(onehot[L][:, j, :], const("iota"), col[:, j:j + 1], None, ALU.is_equal)
                last.then_inc(s_onehot[L], 1)
                v.wait_ge(s_onehot[L], 1)
                link(STT(cum, start, 1.0 / P, nb, ALU.mult, ALU.add))
                c1 = dims(rt[0:1, 0:nb_ * E], nb_, E)
                link(TT(c1, cum[0:1, :].unsqueeze(1).broadcast_to([1, nb_, E]),
                        const("blk")[0:1, 0:nb_].unsqueeze(2).broadcast_to([1, nb_, E]), ALU.is_le))
                es = rt[0:1, 153:153 + nb_]
                link(nc.vector.tensor_reduce(es, c1, AX, ALU.add))
                nc.vector.tensor_copy(be_i[:, BLOCKS_USED:BLOCKS_USED + 1], cum[0:1, E - 1:E])
                TS(be_i[:, 0:nb_], es, float(E - 1), float(FIRST_SLOT[L]), ALU.min, ALU.add).then_inc(s_slots[L], 1)
                v.wait_ge(s_found[L], 1)
                found = rt[:, 0:VALS * nb_]
                first_part = TURNS[L][0][1] * nb_
                link(nc.vector.tensor_copy(found[:, 0:first_part], PS[:, 6, 0:first_part]))
                at = [found[:, nb_ * i:nb_ * (i + 1)] for i in range(VALS)]
                tok = rt[:, 110:110 + nb_]
                link(STT(tok, at[1], float(P), at[0], ALU.mult, ALU.add))
                nc.vector.tensor_copy(gather_i[:, 0:nb_], tok).then_inc(s_index[L], 1)
                link(STT(tok, at[2], const("minus_dump"), tok, ALU.mult, ALU.add))
                TS(add_i[:, 0:nb_], tok, const("dump"), None, ALU.add).then_inc(s_index[L], 1)
                if L == 1:
                    weights()
                    spread(3, 6).then_inc(s_onehot[1], 1)
                    v.wait_ge(s_found[1], 2)
                    link(nc.vector.tensor_copy(found[:, first_part:VALS * nb_], PS[:, 6, first_part:VALS * nb_]))
                link(TT(w_slot[:, 0:nb_], at[5], at[4], ALU.add))
                link(TT(w_slot[:, 0:nb_], w_slot[:, 0:nb_], at[3], ALU.add))

            def experts(L):
                seg = SEG[L]

                def hidden(b, par, k, s):
                    v.wait_ge(s_silu[L], 2 * b + s + 1)
                    part = act[par][:, s * seg:(s + 1) * seg]
                    TT(part, part, PS[:, 2 + s, 0:seg], ALU.mult).then_inc(s_act[L], 1)

                def turned(b, par, k, half):
                    v.wait_ge(s_atr[L], 2 * b + half + 1)
                    if k >= 1:
                        v.wait_ge(s_down[L], b)
                    n = 512 if half == 0 else FCH[L] * P - 512
                    nc.vector.tensor_copy(actT[:, half * 512:half * 512 + n],
                                          PS[:, 4 + half, 0:n]).then_inc(s_atev[L], 1)

                def step(b, par, k):
                    if L == 1 and k < BLOCKS[L] - 1:
                        hidden(b + 1, 1 - par, k + 1, 0)
                    turned(b, par, k, 0)
                    turned(b, par, k, 1)
                    if L == 1 and k < BLOCKS[L] - 1:
                        hidden(b + 1, 1 - par, k + 1, 1)
                    v.wait_ge(s_down[L], b + 1)
                    if k >= 2:
                        v.wait_ge(s_add[L], (b - 1) * 16)
                    TS(ys[par], PS[:, 6, 0:D], w_slot[:, bass.ds(b, 1)], None, ALU.mult).then_inc(s_yev[L], 1)

                def first():
                    if L == 1:
                        hidden(0, 0, 0, 0)
                        hidden(0, 0, 0, 1)

                block_steps(L, v, first, step)

            nc.vector.memset(zeros, 0.0)
            link(nc.vector.memset(h[64:P, NT - 1, :], 0.0))
            nc.vector.memset(mhalf, -0.5)
            v.wait_ge(in_const, 16)
            nc.vector.tensor_copy(vals_b[:, :, :], dims(const("vals"), 2 * NT, VALS)).then_inc(s_clear, 1)
            nc.vector.memset(ones_b[:, :], 1.0)
            nc.vector.memset(mask_b[:, :, :], 0.0)
            v.wait_ge(s_braw, 32)
            link(nc.vector.tensor_copy(bparts[0], braw))
            link(TT(brest, braw, bparts[0], ALU.subtract))
            link(nc.vector.tensor_copy(bparts[1], brest))
            link(TT(brest, brest, bparts[1], ALU.subtract))
            nc.vector.tensor_copy(bparts[2], brest).then_inc(s_bsplit, 3)
            nc.vector.tensor_copy(sel[:, :, :], selraw).then_inc(s_sel, 1)

            def embedded(t):
                v.wait_ge(s_embed, t + 1)
                return nc.vector.tensor_copy(h[0:ROWS[t], t, :], PS[0:ROWS[t], t, 0:D])

            def summed(t):
                v.wait_ge(s_back[t], 16)

            layernorm(0, embedded)
            nc.vector.tensor_copy(tri_b[:, :], const("tri"))
            attention(0, 0)
            layernorm(1, attn_out(0))
            route(0)
            v.wait_ge(s_hb2, 2)
            for t in range(NT):
                n = ROWS[t]
                v.wait_ge(s_shdown, t + 1)
                last = STT(h[0:n, t, :], PS[0:n, SH_BANK[t], 0:D], 0.1, h[0:n, t, :], ALU.mult, ALU.add)
                last.then_inc(s_shev, 1)
            v.wait_ge(s_shev, NT)
            experts(0)
            layernorm(2, summed)
            attention(1, 3)
            layernorm(4, attn_out(1))
            for i in range(2):
                last = nc.vector.memset(act[i][:, HID[1]:FCH[1] * P], 0.0)
            last.then_inc(s_pad, 1)
            route(1)
            experts(1)


def host_layout(x):
    import numpy as np

    def g(name):
        return np.asarray(x[name])

    def kp(w):
        return w.reshape(-1, P, w.shape[1]).transpose(1, 0, 2)

    def flat(w):
        return w.reshape(P, -1)

    o = {}
    img = g("x").reshape(IMGS, 3, 6, 16, 6, 16).transpose(0, 1, 3, 5, 2, 4)
    patches = img.reshape(IMGS, PATCHES, FEAT).transpose(2, 0, 1).reshape(FEAT, TOK)
    o["patches"] = kp(patches)
    o["tok_w"] = kp(g("L0_tok_W"))
    o["wq0"] = flat(kp(g("L0_attn_Wq")))
    o["wk0"] = flat(kp(np.tile(g("L0_attn_Wk"), (1, 4))))
    o["wv0"] = flat(kp(g("L0_attn_Wv")))
    o["wo0"] = flat(kp(g("L0_attn_Wp")))
    o["bp"], o["sbd"] = g("L0_attn_bp"), g("L0_ffn_sbd")
    o["sbu"] = g("L0_ffn_sbu").reshape(8, P).T
    o["wq1"] = flat(kp(g("L1_attn_Wq").T))
    o["wk1"] = flat(kp(g("L1_attn_Wk").T))
    o["wv1"] = flat(kp(g("L1_attn_Wv").T))
    o["wo1"] = flat(kp(g("L1_attn_Wo").T))
    o["gamma_beta"] = np.concatenate([g("L1_attn_ln_gamma").reshape(2, P).T, g("L1_attn_ln_beta").reshape(2, P).T], 1)
    o["gate0"] = kp(g("L0_ffn_gate_w").T)
    o["gbias0"] = g("L0_ffn_gate_bias")
    o["gate1"] = kp(np.concatenate([g("L1_ffn_gate_weight"), g("L1_ffn_new_gate_weight")]).T)
    o["gbias1"] = np.concatenate([np.zeros(8, np.float32), g("L1_ffn_gate_bias")])
    b = np.zeros((8, 1536), np.float32)
    b[:, :1024], b[:, 1024:1280] = g("L0_ffn_bu"), g("L0_ffn_bd")
    o["biases"] = b.reshape(P, 96)

    up0 = np.concatenate([g("L0_ffn_sWu")[None], g("L0_ffn_Wu")])
    dn0 = np.concatenate([g("L0_ffn_sWd")[None], g("L0_ffn_Wd")])
    o["experts0"] = np.stack([np.concatenate([flat(kp(up0[e].T)), flat(kp(dn0[e].T))], 1) for e in range(9)])
    w1 = np.concatenate([g("L1_ffn_w1"), g("L1_ffn_new_w1")])
    w2 = np.concatenate([g("L1_ffn_w2"), g("L1_ffn_new_w2")])
    w3 = np.concatenate([g("L1_ffn_w3"), g("L1_ffn_new_w3")])
    w2t = np.zeros((9, FCH[1] * P, D), np.float32)
    w2t[:, :HID[1]] = w2.transpose(0, 2, 1)
    o["experts1"] = np.stack([np.concatenate([flat(kp(w1[e].T)), flat(kp(w3[e].T)), flat(kp(w2t[e]))], 1)
                              for e in range(9)])

    i, j = np.arange(PATCHES)[:, None], np.arange(PATCHES)[None, :]
    causal = j > i
    slopes = (2.0 ** (-8.0 * np.arange(1, HEADS + 1) / HEADS)).astype(np.float32)
    alibi = (slopes[:, None, None] * (j - i).astype(np.float32) / np.float32(np.sqrt(8.0))).astype(np.float32)
    rel = g("L1_attn_rel")[:, np.clip(i - j, 0, 128)]
    for L, table in enumerate((alibi, rel)):
        slots = np.zeros((P, HEADS, PATCHES), np.float32)
        t = np.where(causal[None], np.float32(NEG), table).transpose(1, 0, 2)
        slots[0:PATCHES], slots[64:64 + PATCHES] = t, t
        o[f"attn_bias{L}"] = slots.reshape(P, -1)

    c = np.zeros((P, NCONST), np.float32)

    def put(name, value):
        at, n = CONST[name]
        c[:, at:at + n] = value

    put("ident", np.eye(P))
    put("tri", np.triu(np.ones((P, P)), 1))
    r = np.arange(P)
    put("vmask", (r[:, None] // PATCHES) == (np.arange(HEADS)[None] % 3))
    hs = np.arange(HEADS)[None]
    put("kmask0", (r[:, None] // DQ[0]) == hs)
    put("kmask1", (r[:, None] // DQ[1]) == hs % HB)
    put("before0", P * np.tril(np.ones((8, 8)), -1).reshape(1, -1))
    put("before1", P * np.tril(np.ones((9, 9)), -1).reshape(1, -1))
    put("thr", P * np.arange(NT)[None])
    put("edge", P * np.arange(18)[None])
    put("iota", r[None] - P)
    vals = np.zeros((P, 2, NT, VALS))
    vals[..., 0], vals[..., 1], vals[..., 2] = r[:, None, None], np.arange(NT)[None, None], 1
    put("vals", vals.reshape(P, -1))
    put("minus_dump", -(TOK + r[:, None]))
    put("dump", TOK + r[:, None])
    put("ids", np.arange(9)[None])
    put("ids99", np.arange(9)[None] - 99)
    put("blk", np.arange(18)[None])
    o["consts"] = c
    s = np.zeros((9, 3, P), np.float32)
    for k in range(9):
        s[k, k // 3] = 1
    o["select"] = s
    return {k: np.ascontiguousarray(w) for k, w in o.items()}


def kernel(**inputs):
    import concourse.bacc as bacc
    from concourse.bass_utils import run_bass_kernel_spmd as run

    nc = bacc.Bacc("TRN2", target_bir_lowering=False, num_devices=1)
    arrays = {f"in_{k}": w for k, w in host_layout(inputs).items()}
    a = {k[3:]: nc.dram_tensor(k, w.shape, F32, kind="ExternalInput").ap() for k, w in arrays.items()}
    a["xn"] = [nc.dram_tensor(f"normalized_{L}", (TOK, D), F32, kind="Internal").ap() for L in range(2)]
    a["values"] = nc.dram_tensor("values", (TOK, D), F32, kind="Internal").ap()
    a["bias_parts"] = nc.dram_tensor("bias_parts", (3, 8 * 1536), BF16, kind="Internal").ap()
    a["sums"] = [nc.dram_tensor("sums_0", (TOK + P, D), F32, kind="Internal").ap(),
                 nc.dram_tensor("out", (TOK + P, D), F32, kind="ExternalOutput").ap()]
    tower(nc, a)
    r = run(nc, [arrays], core_ids=[0])
    return r.results[0]["out"][:TOK].reshape(IMGS, PATCHES, D)
```
